# Optimizing a Trainium2 kernel written in Bass

```python
import numpy as np
import jax
import jax.numpy as jnp

def _softmax(x, axis=-1):
    return jax.nn.softmax(x, axis=axis)

def _gelu(x):
    return jax.nn.gelu(x, approximate=True)

def _silu(x):
    return jax.nn.silu(x)

def _sigmoid(x):
    return jax.nn.sigmoid(x)

def _layernorm(x, axis=-1, eps=1e-05):
    m = jnp.mean(x, axis=axis, keepdims=True)
    v = jnp.var(x, axis=axis, keepdims=True)
    return (x - m) / jnp.sqrt(v + eps)

def _scatter_add(tgt, idx, src, axis=0):
    return tgt.at[idx].add(src)

def _segment_sum(src, seg, n):
    return jax.ops.segment_sum(src, seg, n)
kernel_name = 'mk_adj_resnorm_d4_adj_r2_41ba8f'

def setup_inputs(seed: int=0):
    np.random.seed(seed)
    _w = jnp.asarray

    def _rec_inputs():
        import jax
        import jax.numpy as jnp
        _gk = jax.random.key(seed)
        x = 7.22e-05 + 1 * jax.random.normal(jax.random.fold_in(_gk, 1), (32, 256, 256), jnp.float32)
        _w = (1.0 + jnp.arange(256, dtype=jnp.float32)) ** (-0.5)
        _w = _w / _w.mean()
        _pij = jnp.clip(0.015625 * _w[:, None] * _w[None, :], 0.0, 1.0)
        _a = jax.random.uniform(jax.random.fold_in(_gk, 2), (32, 256, 256)) < _pij
        adj = _a.astype(jnp.int32)
        return (x, adj)
    x, adj = _rec_inputs()

    def _L0_gnn_setup():
        import jax, jax.numpy as jnp
        import numpy as np
        NEG_INF = -1000000000.0
        ALPHA = 0.1
        key = jax.random.key(seed)
        k1, k2, k3, k4, k5 = jax.random.split(key, 5)
        B, N, Din, Dout = (8, 1024, 256, 256)
        features = jax.random.normal(k1, (B, N, Din), dtype=jnp.float32)
        graph = jax.random.randint(k2, (B, N, N), 0, 2, dtype=jnp.int64)
        lim_w = 1.414 * np.sqrt(6.0 / (Din + Dout))
        w = jax.random.uniform(k3, (Din, Dout), jnp.float32, -lim_w, lim_w)
        lim_a = 1.414 * np.sqrt(6.0 / (Dout + 1))
        a1 = jax.random.uniform(k4, (Dout, 1), jnp.float32, -lim_a, lim_a)
        a2 = jax.random.uniform(k5, (Dout, 1), jnp.float32, -lim_a, lim_a)
        return {'features': features, 'graph': graph, 'w': w, 'a1': a1, 'a2': a2}
    _L0_gnn_all = _L0_gnn_setup()
    _L0_gnn_in = {k: v for k, v in _L0_gnn_all.items() if k in ('w', 'a1', 'a2')}
    del _L0_gnn_all

    def _L1_gnn_setup():
        import jax, jax.numpy as jnp
        import numpy as np
        L = 3
        D = 256
        B, N = (8, 512)
        EPS = 1e-05

        def layernorm(x, gamma, beta):
            mu = jnp.mean(x, axis=-1, keepdims=True)
            var = jnp.var(x, axis=-1, keepdims=True)
            return (x - mu) * jax.lax.rsqrt(var + EPS) * gamma + beta
        key = jax.random.key(seed)
        ks = jax.random.split(key, 12)
        s = 1.0 / np.sqrt(D)
        node_features = jax.random.normal(ks[0], (B, N, D), dtype=jnp.float32)
        adjacency_matrix = jax.random.randint(ks[1], (B, N, N), 0, 2, dtype=jnp.int32)
        return {'node_features': node_features, 'adjacency_matrix': adjacency_matrix, 'attn_w': jax.random.normal(ks[2], (L, 2 * D), dtype=jnp.float32) * (1.0 / np.sqrt(2 * D)), 'attn_b': jax.random.normal(ks[3], (L,), dtype=jnp.float32) * 0.01, 'W1': jax.random.normal(ks[4], (L, D, 4 * D), dtype=jnp.float32) * s, 'b1': jnp.zeros((L, 4 * D), dtype=jnp.float32), 'W2': jax.random.normal(ks[5], (L, 4 * D, D), dtype=jnp.float32) * (1.0 / np.sqrt(4 * D)), 'b2': jnp.zeros((L, D), dtype=jnp.float32), 'g1': jnp.ones((L, D), dtype=jnp.float32), 'beta1': jnp.zeros((L, D), dtype=jnp.float32), 'g2': jnp.ones((L, D), dtype=jnp.float32), 'beta2': jnp.zeros((L, D), dtype=jnp.float32)}
    _L1_gnn_all = _L1_gnn_setup()
    _L1_gnn_in = {k: v for k, v in _L1_gnn_all.items() if k in ('attn_w', 'attn_b', 'W1', 'b1', 'W2', 'b2', 'g1', 'beta1', 'g2', 'beta2')}
    del _L1_gnn_all

    def _L2_gnn_setup():
        import jax, jax.numpy as jnp
        import numpy as np
        NEG_SLOPE = 0.2
        key = jax.random.key(seed)
        k1, k2, k3, k4, k5 = jax.random.split(key, 5)
        B, N, H = (8, 512, 256)
        node_features = jax.random.normal(k1, (B, N, H), dtype=jnp.float32)
        adjacency_matrix = jax.random.randint(k2, (B, N, N), 0, 2, dtype=jnp.int32)
        scale = 1.0 / np.sqrt(2 * H)
        attn_w_src = jax.random.uniform(k3, (H,), jnp.float32, -scale, scale)
        attn_w_dst = jax.random.uniform(k4, (H,), jnp.float32, -scale, scale)
        attn_b = jax.random.uniform(k5, (1,), jnp.float32, -scale, scale)
        return {'node_features': node_features, 'adjacency_matrix': adjacency_matrix, 'attn_w_src': attn_w_src, 'attn_w_dst': attn_w_dst, 'attn_b': attn_b}
    _L2_gnn_all = _L2_gnn_setup()
    _L2_gnn_in = {k: v for k, v in _L2_gnn_all.items() if k in ('attn_w_src', 'attn_w_dst', 'attn_b')}
    del _L2_gnn_all

    def _L3_gnn_setup():
        import jax, jax.numpy as jnp
        import numpy as np
        ALPHA = 0.2
        K_NUM = 16
        NEG_INF = -9000000000000000.0
        key = jax.random.key(seed)
        k1, k2, k3, k4 = jax.random.split(key, 4)
        B, N, F_in, F_out = (4, 1024, 256, 256)
        h = jax.random.normal(k1, (B, N, F_in), dtype=jnp.float32)
        adj = jax.random.randint(k2, (B, N, N), 0, 2, dtype=jnp.int32)

        def xavier(k, shape, gain=1.414):
            fan_in, fan_out = (shape[0], shape[1])
            bound = gain * np.sqrt(6.0 / (fan_in + fan_out))
            return jax.random.uniform(k, shape, jnp.float32, -bound, bound)
        W = xavier(k3, (F_in, F_out))
        a = xavier(k4, (2 * F_out, 1))
        return {'h': h, 'adj': adj, 'W': W, 'a': a}
    _L3_gnn_all = _L3_gnn_setup()
    _L3_gnn_in = {k: v for k, v in _L3_gnn_all.items() if k in ('W', 'a')}
    del _L3_gnn_all
    return {'x': x, 'adj': adj, 'L0_gnn_w': _L0_gnn_in['w'], 'L0_gnn_a1': _L0_gnn_in['a1'], 'L0_gnn_a2': _L0_gnn_in['a2'], 'L1_gnn_attn_w': _L1_gnn_in['attn_w'], 'L1_gnn_attn_b': _L1_gnn_in['attn_b'], 'L1_gnn_W1': _L1_gnn_in['W1'], 'L1_gnn_b1': _L1_gnn_in['b1'], 'L1_gnn_W2': _L1_gnn_in['W2'], 'L1_gnn_b2': _L1_gnn_in['b2'], 'L1_gnn_g1': _L1_gnn_in['g1'], 'L1_gnn_beta1': _L1_gnn_in['beta1'], 'L1_gnn_g2': _L1_gnn_in['g2'], 'L1_gnn_beta2': _L1_gnn_in['beta2'], 'L2_gnn_attn_w_src': _L2_gnn_in['attn_w_src'], 'L2_gnn_attn_w_dst': _L2_gnn_in['attn_w_dst'], 'L2_gnn_attn_b': _L2_gnn_in['attn_b'], 'L3_gnn_W': _L3_gnn_in['W'], 'L3_gnn_a': _L3_gnn_in['a']}

def reference(x, adj, L0_gnn_w, L0_gnn_a1, L0_gnn_a2, L1_gnn_attn_w, L1_gnn_attn_b, L1_gnn_W1, L1_gnn_b1, L1_gnn_W2, L1_gnn_b2, L1_gnn_g1, L1_gnn_beta1, L1_gnn_g2, L1_gnn_beta2, L2_gnn_attn_w_src, L2_gnn_attn_w_dst, L2_gnn_attn_b, L3_gnn_W, L3_gnn_a):
    import jax
    import jax.numpy as jnp

    def _L0_gnn_ref(features, graph, w, a1, a2):
        import jax, jax.numpy as jnp
        import numpy as np
        NEG_INF = -1000000000.0
        ALPHA = 0.1
        hidden = jnp.einsum('bni,io->bno', features, w)
        s1 = hidden @ a1
        s2 = hidden @ a2
        e = jax.nn.leaky_relu(s1 + jnp.swapaxes(s2, 1, 2), negative_slope=ALPHA)
        e = jnp.where(graph == 0, NEG_INF, e)
        attn = jax.nn.softmax(e, axis=-1)
        h_prime = jnp.einsum('bij,bjo->bio', attn, hidden)
        return jax.nn.elu(h_prime)

    def _L1_gnn_ref(node_features, adjacency_matrix, attn_w, attn_b, W1, b1, W2, b2, g1, beta1, g2, beta2):
        import jax, jax.numpy as jnp
        import numpy as np
        L = 3
        D = 256
        B, N = (8, 512)
        EPS = 1e-05

        def layernorm(x, gamma, beta):
            mu = jnp.mean(x, axis=-1, keepdims=True)
            var = jnp.var(x, axis=-1, keepdims=True)
            return (x - mu) * jax.lax.rsqrt(var + EPS) * gamma + beta
        n = adjacency_matrix.shape[-1]
        mask = adjacency_matrix.astype(jnp.float32) + jnp.eye(n, dtype=jnp.float32) > 0
        x = node_features
        d = x.shape[-1]
        for l in range(attn_w.shape[0]):
            si = x @ attn_w[l, :d]
            sj = x @ attn_w[l, d:]
            scores = si[:, :, None] + sj[:, None, :] + attn_b[l]
            scores = jnp.where(scores >= 0, scores, 0.2 * scores)
            scores = jnp.where(mask, scores, -jnp.inf)
            attn = jax.nn.softmax(scores, axis=-1)
            agg = jnp.einsum('bij,bjd->bid', attn, x)
            h = layernorm(x + agg, g1[l], beta1[l])
            ff = jax.nn.gelu(h @ W1[l] + b1[l], approximate=False) @ W2[l] + b2[l]
            x = layernorm(h + ff, g2[l], beta2[l])
        return x

    def _L2_gnn_ref(node_features, adjacency_matrix, attn_w_src, attn_w_dst, attn_b):
        import jax, jax.numpy as jnp
        import numpy as np
        NEG_SLOPE = 0.2
        B, N, H = node_features.shape
        s_src = jnp.einsum('bnh,h->bn', node_features, attn_w_src)
        s_dst = jnp.einsum('bnh,h->bn', node_features, attn_w_dst)
        scores = s_src[:, :, None] + s_dst[:, None, :] + attn_b[0]
        scores = jax.nn.leaky_relu(scores, negative_slope=NEG_SLOPE)
        adj = adjacency_matrix.astype(jnp.float32) + jnp.eye(N, dtype=jnp.float32)[None]
        scores = jnp.where(adj == 0, -jnp.inf, scores)
        attn = jax.nn.softmax(scores, axis=-1)
        return jnp.einsum('bij,bjh->bih', attn, node_features)

    def _L3_gnn_ref(h, adj, W, a):
        import jax, jax.numpy as jnp
        import numpy as np
        ALPHA = 0.2
        K_NUM = 16
        NEG_INF = -9000000000000000.0
        F_out = W.shape[1]
        Wh = jnp.einsum('bnf,fo->bno', h, W)
        a1, a2 = (a[:F_out, 0], a[F_out:, 0])
        e_src = Wh @ a1
        e_dst = Wh @ a2
        e = e_src[:, :, None] + e_dst[:, None, :]
        e = jnp.where(e > 0, e, ALPHA * e)
        e = jnp.where(adj > 0, e, NEG_INF)
        attention = jax.nn.softmax(e, axis=2)
        topk_vals = jax.lax.top_k(attention, K_NUM)[0]
        kth = topk_vals[:, :, -1:]
        attention = jnp.where(attention < kth, 0.0, attention)
        h_prime = jnp.einsum('bij,bjo->bio', attention, Wh)
        return jax.nn.elu(h_prime)
    x = _layernorm(x + _L0_gnn_ref(x, adj, L0_gnn_w, L0_gnn_a1, L0_gnn_a2), axis=-1)
    x = _layernorm(x + _L1_gnn_ref(x, adj, L1_gnn_attn_w, L1_gnn_attn_b, L1_gnn_W1, L1_gnn_b1, L1_gnn_W2, L1_gnn_b2, L1_gnn_g1, L1_gnn_beta1, L1_gnn_g2, L1_gnn_beta2), axis=-1)
    x = _layernorm(x + _L2_gnn_ref(x, adj, L2_gnn_attn_w_src, L2_gnn_attn_w_dst, L2_gnn_attn_b), axis=-1)
    x = _layernorm(x + _L3_gnn_ref(x, adj, L3_gnn_W, L3_gnn_a), axis=-1)
    return x

_drawn_inputs = setup_inputs


def setup_inputs(seed=0):
    import zlib

    import numpy as np

    out = dict(_drawn_inputs(seed))
    spreads = {'L1_gnn_b1': (0.0, 0.1),
     'L1_gnn_b2': (0.0, 0.1),
     'L1_gnn_g1': (1.0, 0.2),
     'L1_gnn_beta1': (0.0, 0.1),
     'L1_gnn_g2': (1.0, 0.2),
     'L1_gnn_beta2': (0.0, 0.1)}
    factors = {'L1_gnn_attn_b': 64.0, 'L2_gnn_attn_w_src': 3.017}
    for name, (base, spread) in spreads.items():
        noise = np.random.default_rng([zlib.crc32(name.encode()), seed]).standard_normal(out[name].shape)
        drawn = base * np.exp(spread * noise) if base else spread * noise
        out[name] = jnp.asarray(drawn.astype(out[name].dtype))
    for name, factor in factors.items():
        out[name] = (out[name] * factor).astype(out[name].dtype)
    return out
```

```python
import concourse.bass as bass
from concourse import mybir
from contextlib import ExitStack

F32 = mybir.dt.float32
F32R = mybir.dt.float32r
I32 = mybir.dt.int32
I8 = mybir.dt.int8
ALU = mybir.AluOpType
ACT = mybir.ActivationFunctionType

P = 128
GRAPHS, N, D = 32, 256, 256
PAIRS = GRAPHS // 2
T = 2 * N // P
KT = D // P
TOK = 2 * N
LAYERS, FF = 3, 1024
FT = FF // P
BLOCKS = 6
UNITS = BLOCKS * PAIRS
FFN = (1, 2, 3)
PROJ = (0, 5)
TOPK = 5
ALPHA = (0.1, 0.2, 0.2, 0.2, 0.2, 0.2)
EPS = 1e-5
BIG = 2.0 ** 64
FFN0 = FFN[0] * PAIRS
LAST = UNITS - PAIRS

V_ATT, V_B1, V_G1, V_BETA1, V_SRC, V_DST, V_ROWS = 0, 12, 36, 42, 48, 50, 52


def graph_stack(nc, x, adj, w0, a0_src, a0_dst, attn_w, attn_b, w1, b1, w2, b2, g1, beta1, g2, beta2,
                l2_src, l2_dst, l2_b, w3, a3, out):
    x_t = x.rearrange("b (i p) d -> p (b i) d", p=P)
    adj_t = adj.rearrange("b (i p) j -> p (b i) j", p=P)
    out_t = out.rearrange("b (i p) d -> p (b i) d", p=P)
    x_outer = nc.dram_tensor("x_outer", (P, PAIRS * T, D), F32, kind="Internal").ap()
    w_split = nc.dram_tensor("w_split", (LAYERS, 4, P, KT * FF), F32, kind="Internal").ap()

    ctx = ExitStack()
    with ctx:
        def sb(name, shape, dt=F32):
            return ctx.enter_context(nc.sbuf_tensor(name, shape, dt))

        def sem(name):
            return ctx.enter_context(nc.semaphore(name))

        state = sb("state", [P, PAIRS * T, D])
        edges = sb("edges", [P, PAIRS * T, N], I8)
        w1_hi = sb("w1_hi", [P, KT, FF], F32R)
        w1_lo = sb("w1_lo", [P, KT, FF], F32R)
        w2_hi = sb("w2_hi", [P, FT, D], F32R)
        w2_lo = sb("w2_lo", [P, FT, D], F32R)
        w_proj = sb("w_proj", [P, KT, D])
        a_rows = sb("a_rows", [P, 2, D])
        wa = sb("wa", [P, 2, 2, KT])
        dst_rep = sb("dst_rep", [P, 2, KT, P])
        vec_rows = sb("vec_rows", [V_ROWS, P])
        vec = sb("vec", [P, V_ROWS])
        score_b = sb("score_b", [P, BLOCKS])
        norm_w = sb("norm_w", [P, LAYERS, 4, D])
        ident = sb("ident", [P, P])
        neg_half = sb("neg_half", [P, T])
        x_front = sb("x_front", [P, T, D])
        x_mix = sb("x_mix", [P, T, D])
        xT = sb("xT", [P, KT, TOK])
        adj_mask = sb("adj_mask", [P, T, N], I8)
        loop_mask = sb("loop_mask", [P, T, N], I8)
        masked = sb("masked", [P, T, N])
        attn = sb("attn", [P, T, N])
        attnT = sb("attnT", [P, 2, KT, N])
        y = sb("y", [P, T, D])
        values = sb("values", [P, T, D])
        h_hi = sb("h_hi", [P, KT, TOK], F32R)
        h_lo = sb("h_lo", [P, KT, TOK], F32R)
        h_res = sb("h_res", [P, T, D])
        act = sb("act", [P, 2, TOK])
        act_hi = sb("act_hi", [P, 4, TOK], F32R)
        act_lo = sb("act_lo", [P, 4, TOK], F32R)
        y2 = sb("y2", [P, T, D])
        s_col = sb("s_col", [P, T])
        row_max = sb("row_max", [P, T])
        z_max = sb("z_max", [P, T])
        m_col = sb("m_col", [P, T])
        exp_bias = sb("exp_bias", [P, 2, T])
        row_sum = sb("row_sum", [P, T])
        inv_sum = sb("inv_sum", [P, T])
        top_a = sb("top_a", [P, T, 8])
        top_b = sb("top_b", [P, T, 8])
        stats = [sb(f"stats{i}", [P, T, 6]) for i in range(3)]
        mean_var = [sb(f"mean_var{i}", [P, T, 2]) for i in range(3)]
        var_eps = [sb(f"var_eps{i}", [P, T]) for i in range(3)]
        rstd = [sb(f"rstd{i}", [P, T]) for i in range(3)]

        adj_in = act[:, :, :].bitcast(I32).rearrange("p a (t j) -> p (a t) j", j=N)
        hT = attn[:, :, :].rearrange("p (u a) n -> p u (a n)", u=KT)
        x_saved = values
        neg = y2
        pos = h_res

        bank = [ctx.enter_context(nc.psum_tensor(f"bank{i}", [P, 512], F32)) for i in range(8)]
        TR = bank[0:2]
        ACC = bank[2:4]
        HID = bank[4:8]
        MIXB, S_BANK, D_BANK = HID[0:2], HID[2], HID[3]

        consts_in = sem("consts_in")
        wproj_in = sem("wproj_in")
        chunk_in = [sem(f"chunk_in{i}") for i in range(2)]
        chunk_split = sem("chunk_split")
        chunk_part = sem("chunk_part")
        split_saved = sem("split_saved")
        w1_in = sem("w1_in")
        w2_in = sem("w2_in")
        ident_ready = sem("ident_ready")
        vec_mm = sem("vec_mm")
        vec_ready = sem("vec_ready")
        wa_ready = sem("wa_ready")
        prep_ready = sem("prep_ready")
        bb_ready = sem("bb_ready")
        xs_in = sem("xs_in")
        xm_in = sem("xm_in")
        mask_in = sem("mask_in")
        adj_loaded = sem("adj_loaded")
        mask_made = sem("mask_made")
        loops_made = sem("loops_made")
        edges_saved = sem("edges_saved")
        y_saved = sem("y_saved")
        y2_saved = sem("y2_saved")
        outer_saved = sem("outer_saved")
        saved_in = sem("saved_in")
        out_saved = sem("out_saved")
        x_turned = sem("x_turned")
        xT_ready = sem("xT_ready")
        scored = sem("scored")
        projected = sem("projected")
        values_ready = sem("values_ready")
        s_ready = sem("s_ready")
        max_ready = sem("max_ready")
        z_ready = sem("z_ready")
        m_ready = sem("m_ready")
        bias_ready = sem("bias_ready")
        exps_done = sem("exps_done")
        weights_made = sem("weights_made")
        inv_ready = sem("inv_ready")
        top_step = sem("top_step")
        attn_ready = sem("attn_ready")
        attn_turned = sem("attn_turned")
        attnT_a = sem("attnT_a")
        attnT_d = sem("attnT_d")
        mixed = sem("mixed")
        elu_parts = sem("elu_parts")
        elu_exp = sem("elu_exp")
        elu_sum = sem("elu_sum")
        y_ready = sem("y_ready")
        stats_done = [sem(f"stats_done{i}") for i in range(3)]
        moments = [sem(f"moments{i}") for i in range(3)]
        var_ready = [sem(f"var_ready{i}") for i in range(3)]
        rstd_ready = [sem(f"rstd_ready{i}") for i in range(3)]
        normed = [sem(f"normed{i}") for i in range(3)]
        n_turned = sem("n_turned")
        hT_ready = sem("hT_ready")
        h_hi_ready = sem("h_hi_ready")
        h_ready = sem("h_ready")
        res_scaled = sem("res_scaled")
        res_ready = sem("res_ready")
        hid_done = sem("hid_done")
        act_ready = sem("act_ready")
        act_hi_ready = sem("act_hi_ready")
        act_split = sem("act_split")
        ff_done = sem("ff_done")
        y2_ready = sem("y2_ready")
        x_scaled = sem("x_scaled")
        x_ready = sem("x_ready")
        outer_added = sem("outer_added")
        taken = sem("taken")

        block = ctx.enter_context(nc.Block())

        def rows(pair):
            return bass.ds(pair * T, T)

        def words(w):
            return w[:, :, :].rearrange("p k f -> p (k f)").bitcast(F32)

        def columns(b, which):
            if b in PROJ:
                return wa[:, PROJ.index(b), which, :]
            if b in FFN:
                c = V_ATT + ((b - 1) * 2 + which) * KT
                return vec[:, c:c + KT]
            c = V_DST if which else V_SRC
            return vec[:, c:c + KT]

        def proj_unit(g, b):
            return g if b == 0 else g - LAST + PAIRS

        def y_store(g, b):
            return g - {0: 0, 4: 3 * PAIRS, 5: 3 * PAIRS}[b]

        def drive(eng, step):
            def of(g):
                return int(g // PAIRS) if 0 <= g < UNITS else None

            def straight(k):
                step(k, of(k - 1), of(k), of(k + 1), of(k + 2))

            for k in (-2, -1):
                straight(k)
            for b in range(BLOCKS):
                first = 3 if b == 0 else 1
                for p in range(first):
                    straight(b * PAIRS + p)
                with eng.Fori(first, PAIRS - 3) as p:
                    step(p + b * PAIRS, b, b, b, b)
                for p in range(PAIRS - 3, PAIRS):
                    straight(b * PAIRS + p)

        def known(g, least=1):
            return not isinstance(g, int) or g >= least

        @block.sync
        def _(sp):
            ld = nc.allow_non_contiguous_dma(reason="small constants")
            ld.__enter__()
            sp.dma_start(x_front[:, :, :], x_t[:, 0:T, :]).then_inc(xs_in, 16)
            for base, src in ((V_ATT, attn_w.rearrange("l (r q) -> (l r) q", q=P)),
                              (V_B1, b1.rearrange("l (r q) -> (l r) q", q=P)),
                              (V_G1, g1.rearrange("l (r q) -> (l r) q", q=P)),
                              (V_BETA1, beta1.rearrange("l (r q) -> (l r) q", q=P)),
                              (V_SRC, l2_src.rearrange("(r q) -> r q", q=P)),
                              (V_DST, l2_dst.rearrange("(r q) -> r q", q=P))):
                sp.dma_start(vec_rows[base:base + src.shape[0], :], src).then_inc(consts_in, 16)
            sp.dma_start(score_b[:, 1:4], attn_b.unsqueeze(0).to_broadcast([P, LAYERS])).then_inc(consts_in, 16)
            sp.dma_start(score_b[:, 4:5], l2_b.unsqueeze(0).to_broadcast([P, 1])).then_inc(consts_in, 16)
            for i, src in enumerate((g1, beta1, g2, beta2)):
                for l in range(LAYERS):
                    sp.dma_start(norm_w[:, l, i, :], src[l:l + 1, :].to_broadcast([P, D])).then_inc(consts_in, 16)
            for l in range(LAYERS):
                sp.dma_start(y[:, l, :], b2[l:l + 1, :].to_broadcast([P, D])).then_inc(consts_in, 16)
            sp.dma_start(w_proj[:, :, :], w0.rearrange("(t p) n -> p t n", p=P)).then_inc(wproj_in, 16)
            for i, src in enumerate((a0_src, a0_dst)):
                sp.dma_start(a_rows[:, i, :], src.rearrange("n o -> o n").to_broadcast([P, D])).then_inc(wproj_in, 16)
            n = 0
            for l in reversed(range(LAYERS)):
                for q in range(4):
                    if n >= 2:
                        sp.wait_ge(chunk_split, n - 1)
                    dst = (h_res, y2)[n % 2]
                    src = w1[l, (q % 2) * P:(q % 2 + 1) * P, :] if q < 2 else \
                        w2[l, (q % 2) * 4 * P:(q % 2 + 1) * 4 * P, :].rearrange("(t p) n -> p t n", p=P)
                    view = dst[:, :, :].rearrange("p t n -> p (t n)") if q < 2 else dst[:, :, :]
                    sp.dma_start(view, src).then_inc(chunk_in[n % 2], 16)
                    n += 1
                if l:
                    sp.wait_ge(chunk_split, n)
                    for i, part in enumerate((w1_hi, w1_lo, w2_hi, w2_lo)):
                        sp.dma_start(w_split[l, i], words(part)).then_inc(split_saved, 16)
            ld.__exit__(None, None, None)

            def load_mask(g, b):
                if known(g):
                    sp.wait_ge(max_ready, g)
                if b == 1 and isinstance(g, int):
                    sp.wait_ge(loops_made, min(g, PAIRS))
                sp.wait_ge(edges_saved, 16 * (g - b * PAIRS + 1))
                sp.sem_inc(taken, 1)
                sp.dma_start(adj_mask[:, :, :], edges[:, rows(g - b * PAIRS), :]).then_inc(mask_in, 16)

            def load_adj(g, b):
                a = proj_unit(g, b)
                if known(a):
                    sp.wait_ge(mask_made, a)
                if b == TOPK and isinstance(g, int):
                    sp.wait_ge(act_split, FT * 3 * PAIRS)
                sp.sem_inc(taken, 1)
                sp.dma_start(adj_in, adj_t[:, rows(g - b * PAIRS), :]).then_inc(adj_loaded, 16)

            def load_x(g, b, dst, done):
                if b - 1 in FFN:
                    sp.wait_ge(y2_saved, (g - PAIRS - FFN0 + 1) * 16)
                elif b > 0:
                    sp.wait_ge(y_saved, (y_store(g - PAIRS, b - 1) + 1) * 16)
                sp.sem_inc(taken, 1)
                src = x_t if b == 0 else state
                sp.dma_start(dst[:, :, :], src[:, rows(g - b * PAIRS), :]).then_inc(done, 16)

            def step(k, prev, cur, mid, front):
                if front in PROJ:
                    load_adj(k + 2, front)
                elif front is not None:
                    load_mask(k + 2, front)
                if prev in FFN:
                    if prev == FFN[-1]:
                        sp.wait_ge(normed[2], k - 1 - FFN[-1] * PAIRS + 1)
                    else:
                        sp.wait_ge(x_ready, k - 1 - FFN0 + 1)
                    sp.sem_inc(taken, 1)
                    sp.dma_start(state[:, rows(k - 1 - prev * PAIRS), :], y2[:, :, :]).then_inc(y2_saved, 16)
                if cur == FFN[-1]:
                    if known(k, FFN[-1] * PAIRS + 1):
                        sp.wait_ge(outer_added, k - FFN[-1] * PAIRS)
                    else:
                        sp.wait_ge(outer_saved, 16 * PAIRS)
                    sp.sem_inc(taken, 1)
                    sp.dma_start(x_saved[:, :, :], x_outer[:, rows(k - cur * PAIRS), :]).then_inc(saved_in, 16)
                if isinstance(k, int) and cur in FFN and k % PAIRS == 0 and cur != FFN[0]:
                    l = cur - 1
                    sp.wait_ge(ff_done, FT * (k - FFN0))
                    sp.dma_start(words(w2_hi), w_split[l, 2]).then_inc(w2_in, 16)
                    sp.dma_start(words(w2_lo), w_split[l, 3]).then_inc(w2_in, 16)
                if isinstance(k, int) and cur in FFN and k % PAIRS == PAIRS - 1 and cur != FFN[-1]:
                    l = cur
                    sp.wait_ge(split_saved, 16 * 4 * (LAYERS - 1))
                    sp.wait_ge(hid_done, FT * (k - FFN0 + 1))
                    sp.dma_start(words(w1_hi), w_split[l, 0]).then_inc(w1_in, 16)
                    sp.dma_start(words(w1_lo), w_split[l, 1]).then_inc(w1_in, 16)
                if isinstance(k, int) and k == 2 * PAIRS:
                    sp.wait_ge(projected, PAIRS)
                    sp.wait_ge(wa_ready, 2)
                    sp.dma_start(w_proj[:, :, :], w3.rearrange("(t p) n -> p t n", p=P)).then_inc(wproj_in, 16)
                    sp.dma_start(a_rows[:, :, :], a3.rearrange("(h n) o -> o h n", h=2).to_broadcast([P, 2, D]))\
                      .then_inc(wproj_in, 16)
                ahead = (k + 3) // PAIRS if isinstance(k, int) else front
                if ahead is not None and (not isinstance(k, int) or k + 3 < UNITS):
                    sp.wait_ge(x_turned, 2 * (k + 3))
                    load_x(k + 3, ahead, x_front, xs_in)
                if cur not in FFN and mid is not None:
                    if cur is not None:
                        sp.wait_ge(y_ready, k + 1)
                        sp.sem_inc(taken, 1)
                    load_x(k + 1, mid, x_mix, xm_in)
                if cur is not None and cur not in FFN:
                    sp.wait_ge(normed[0], k + 1)
                    sp.sem_inc(taken, 1)
                    where = rows(k - cur * PAIRS)
                    if cur == BLOCKS - 1:
                        sp.dma_start(out_t[:, where, :], y[:, :, :]).then_inc(out_saved, 16)
                    else:
                        sp.dma_start(state[:, where, :], y[:, :, :]).then_inc(y_saved, 16)
                    if cur == 0:
                        sp.dma_start(x_outer[:, where, :], y[:, :, :]).then_inc(outer_saved, 16)
                if mid == 0:
                    sp.wait_ge(loops_made, k + 2)
                    sp.sem_inc(taken, 1)
                    sp.dma_start(edges[:, rows(k + 1), :], loop_mask[:, :, :]).then_inc(edges_saved, 16)
                if mid in FFN and front is not None:
                    sp.wait_ge(y_ready, k + 2)
                    load_x(k + 2, front, x_mix, xm_in)

            drive(sp, step)
            sp.wait_ge(out_saved, 16 * PAIRS)
            sp.wait_ge(outer_saved, 16 * PAIRS)

        @block.gpsimd
        def _(pool):
            pool.memset(neg_half[:, :], -0.5)
            pool.memset(ident[:, :], 0.0).then_inc(ident_ready, 1)
            pool.wait_ge(ident_ready, 1)
            pool.affine_select(out=ident[:, :], in_=ident[:, :], compare_op=ALU.not_equal, fill=1.0, base=0,
                               pattern=[[-1, P]], channel_multiplier=1).then_inc(ident_ready, 1)
            pool.wait_ge(ident_ready, 2)
            pool.wait_ge(consts_in, 16 * (8 + 5 * LAYERS))
            pool.tensor_tensor(norm_w[:, :, 1, :], norm_w[:, :, 1, :], y[:, 0:LAYERS, :], ALU.add).then_inc(bb_ready, 1)
            pool.wait_ge(bb_ready, 1)

            def rsqrt(i, n):
                pool.wait_ge(var_ready[i], n + 1)
                pool.tensor_tensor(rstd[i][:, :], var_eps[i][:, :], neg_half[:, :], ALU.pow).then_inc(rstd_ready[i], 1)

            def wide(l, i):
                return norm_w[:, l:l + 1, i, :].to_broadcast([P, T, D])

            def step(k, prev, cur, mid, front):
                if mid == 0:
                    g = k + 1
                    pool.wait_ge(mask_made, g + 1)
                    if known(g):
                        pool.wait_ge(edges_saved, 16 * g)
                    pool.sem_inc(taken, 1)
                    pool.affine_select(out=loop_mask[:, :, :].rearrange("p (b i) j -> p b i j", b=2),
                                       in_=adj_mask[:, :, :].rearrange("p (b i) j -> p b i j", b=2),
                                       compare_op=ALU.not_equal, fill=0.0, base=0,
                                       pattern=[[0, 2], [P, KT], [-1, N]], channel_multiplier=1)\
                        .then_inc(loops_made, 1)
                if prev in FFN:
                    rsqrt(1, k - 1 - FFN0)
                if cur in FFN:
                    f = k - FFN0
                    pool.wait_ge(normed[0], k + 1)
                    if known(f):
                        pool.wait_ge(y2_ready, f)
                    pool.tensor_tensor(h_res[:, :, :], y[:, :, :], wide(cur - 1, 0), ALU.mult).then_inc(res_scaled, 1)
                    pool.wait_ge(res_scaled, f + 1)
                    pool.tensor_tensor(h_res[:, :, :], h_res[:, :, :], wide(cur - 1, 1), ALU.add).then_inc(res_ready, 1)
                if prev in FFN:
                    f = k - 1 - FFN0
                    pool.wait_ge(normed[1], f + 1)
                    pool.tensor_tensor(y2[:, :, :], y2[:, :, :], wide(prev - 1, 2), ALU.mult).then_inc(x_scaled, 1)
                    pool.wait_ge(x_scaled, f + 1)
                    pool.tensor_tensor(y2[:, :, :], y2[:, :, :], wide(prev - 1, 3), ALU.add).then_inc(x_ready, 1)
                    if prev == FFN[-1]:
                        n = k - 1 - prev * PAIRS
                        pool.wait_ge(x_ready, f + 1)
                        pool.wait_ge(saved_in, 16 * (n + 1))
                        pool.tensor_tensor(y2[:, :, :], y2[:, :, :], x_saved[:, :, :], ALU.add).then_inc(outer_added, 1)
                if cur is not None and cur not in FFN:
                    rsqrt(0, k)
                if mid in FFN:
                    rsqrt(0, k + 1)
                if prev == FFN[-1]:
                    rsqrt(2, k - 1 - prev * PAIRS)

            drive(pool, step)

        @block.scalar
        def _(act_e):
            act_e.wait_ge(vec_ready, 1)

            def gelu(k, cur, ft):
                f = k - FFN0
                act_e.wait_ge(hid_done, FT * f + ft + 1)
                if ft >= 2 or known(f):
                    act_e.wait_ge(act_split, FT * f + ft - 1)
                c = V_B1 + (cur - 1) * FT + ft
                act_e.activation(act[:, ft % 2, :], HID[ft % 4][:, :], ACT.Gelu, bias=vec[:, c:c + 1])\
                    .then_inc(act_ready, 1)

            def exps(g, cur, mid):
                act_e.wait_ge(bias_ready, g + 1)
                if cur in FFN:
                    act_e.wait_ge(h_ready, g - FFN0)
                elif known(g):
                    act_e.wait_ge(attn_turned, 2 * g)
                for t in range(T):
                    act_e.activation(attn[:, t, :], masked[:, t, :], ACT.Exp, bias=exp_bias[:, 0, t:t + 1])
                for t in range(T):
                    last = act_e.activation(masked[:, t, :], masked[:, t, :], ACT.Exp,
                                            bias=exp_bias[:, 1, t:t + 1], scale=ALPHA[mid])
                last.then_inc(exps_done, 1)

            def copy_xT(g, front):
                for u in range(KT):
                    act_e.wait_ge(x_turned, 2 * g + u + 1)
                    if known(g) and u == 0:
                        act_e.wait_ge(scored, g)
                        if front in PROJ and known(proj_unit(g, front)):
                            act_e.wait_ge(projected, proj_unit(g, front))
                        elif front == 1 and isinstance(g, int):
                            act_e.wait_ge(projected, PAIRS)
                    act_e.activation(xT[:, u, :], TR[u][:, :], ACT.Copy).then_inc(xT_ready, 1)

            def step(k, prev, cur, mid, front):
                g = k + 1
                if cur in FFN:
                    for ft in range(4):
                        gelu(k, cur, ft)
                elif front is not None:
                    copy_xT(k + 2, front)
                if mid is not None:
                    exps(g, cur, mid)
                if cur in PROJ:
                    act_e.wait_ge(elu_parts, proj_unit(k, cur) + 1)
                    act_e.activation(neg[:, :, :], neg[:, :, :], ACT.Exp).then_inc(elu_exp, 1)
                if cur in FFN:
                    for ft in range(4, FT - 1):
                        gelu(k, cur, ft)
                if mid is not None:
                    act_e.wait_ge(attn_turned, 2 * g + 1)
                    if known(g):
                        act_e.wait_ge(mixed, 2 * g)
                    act_e.activation(attnT[:, 0, :, :].rearrange("p a n -> p (a n)"), TR[0][:, :], ACT.Copy)\
                        .then_inc(attnT_a, 1)
                if cur in FFN:
                    gelu(k, cur, FT - 1)
                if cur in FFN and front is not None:
                    copy_xT(k + 2, front)
                if mid in FFN:
                    f = g - FFN0
                    for u in range(KT):
                        act_e.wait_ge(n_turned, 2 * f + u + 1)
                        cg, cb = V_G1 + (mid - 1) * KT + u, V_BETA1 + (mid - 1) * KT + u
                        act_e.activation(hT[:, u, :], TR[u][:, :], ACT.Identity, bias=vec[:, cb:cb + 1],
                                         scale=vec[:, cg:cg + 1]).then_inc(hT_ready, 1)
                if front in PROJ:
                    a = proj_unit(k + 2, front)
                    act_e.wait_ge(projected, a + 1)
                    if known(k + 2):
                        act_e.wait_ge(mixed, 2 * (k + 2))
                    if front == TOPK and isinstance(k, int):
                        act_e.wait_ge(outer_added, PAIRS)
                    for c in range(2):
                        act_e.activation(values[:, 2 * c:2 * c + 2, :].rearrange("p a n -> p (a n)"), ACC[c][:, :],
                                         ACT.Copy).then_inc(values_ready, 1)

            drive(act_e, step)

        @block.vector
        def _(dve):
            dve.memset(score_b[:, 0:1], 0.0)
            dve.memset(score_b[:, 5:6], 0.0)
            dve.wait_ge(vec_mm, 1)
            dve.tensor_copy(vec[:, :], TR[0][:, 0:V_ROWS]).then_inc(vec_ready, 1)

            def project_vectors(i):
                dve.wait_ge(wproj_in, 16 * (3 if i == 0 else 5))
                for j in range(2):
                    for c in range(KT):
                        last = dve.tensor_tensor_reduce(out=masked[:, 2 * j + c, :], in0=w_proj[:, c, :], in1=a_rows[:, j, :],
                                                        scale=1.0, scalar=0.0, op0=ALU.mult, op1=ALU.add,
                                                        accum_out=wa[:, i, j, c:c + 1])
                last.then_inc(wa_ready, 1)
                dve.wait_ge(wa_ready, 2 * i + 1)

            def prepare(b):
                if b == TOPK:
                    dve.wait_ge(exps_done, (b - 1) * PAIRS + PAIRS - 1)
                    dve.wait_ge(weights_made, (b - 1) * PAIRS + PAIRS - 1)
                    project_vectors(1)
                if b >= 2:
                    dve.wait_ge(scored, (b - 1) * PAIRS)
                dve.tensor_scalar(dst_rep[:, b % 2, :, :], columns(b, 1).unsqueeze(2).to_broadcast([P, KT, P]),
                                  1.0 / BIG, None, ALU.mult).then_inc(prep_ready, 1)

            dve.wait_ge(bb_ready, 1)
            project_vectors(0)
            dve.sem_inc(wa_ready, 1)
            dve.wait_ge(vec_ready, 1)
            prepare(0)
            prepare(1)
            n = 0
            for l in reversed(range(LAYERS)):
                for q in range(4):
                    dve.wait_ge(chunk_in[n % 2], 16 * (n // 2 + 1))
                    if q == 0 and l < LAYERS - 1:
                        dve.wait_ge(split_saved, 16 * 4 * (LAYERS - 1 - l))
                    raw = (h_res, y2)[n % 2][:, :, :].rearrange("p t n -> p (t n)")
                    if q < 2:
                        hi, lo = w1_hi[:, q, :], w1_lo[:, q, :]
                    else:
                        hi = w2_hi[:, 4 * (q - 2):4 * (q - 1), :].rearrange("p t n -> p (t n)")
                        lo = w2_lo[:, 4 * (q - 2):4 * (q - 1), :].rearrange("p t n -> p (t n)")
                    dve.tensor_copy(hi, raw).then_inc(chunk_part, 1)
                    n += 1
                    dve.wait_ge(chunk_part, n)
                    dve.tensor_tensor(lo, raw, hi.bitcast(F32), ALU.subtract).then_inc(chunk_split, 1)

            def layer_norm(i, n, buf):
                for t in range(T):
                    last = dve.bn_stats(stats[i][:, t, :], buf[:, t, :])
                last.then_inc(stats_done[i], 1)
                dve.wait_ge(stats_done[i], n + 1)
                dve.sem_inc(taken, 1)
                for t in range(T):
                    last = dve.bn_aggr(mean_var[i][:, t, :], stats[i][:, t, :])
                last.then_inc(moments[i], 1)
                dve.wait_ge(moments[i], n + 1)
                dve.tensor_scalar(var_eps[i][:, :], mean_var[i][:, :, 1], EPS, None, ALU.add).then_inc(var_ready[i], 1)

            def finish(i, n, buf):
                dve.wait_ge(rstd_ready[i], n + 1)
                for t in range(T):
                    last = dve.tensor_scalar(buf[:, t, :], buf[:, t, :], mean_var[i][:, t, 0:1], rstd[i][:, t:t + 1],
                                             ALU.subtract, ALU.mult)
                last.then_inc(normed[i], 1)

            def scores(g, cur, mid):
                if mid in PROJ:
                    a = proj_unit(g, mid)
                    dve.wait_ge(adj_loaded, 16 * (a + 1))
                    if known(g):
                        dve.wait_ge(max_ready, g)
                    if mid == 0 and known(g):
                        dve.wait_ge(loops_made, g)
                    dve.tensor_scalar(adj_mask[:, :, :], adj_in, 1.0, -1.0, ALU.is_lt, ALU.mult).then_inc(mask_made, 1)
                dve.wait_ge(scored, g + 1)
                if known(g):
                    dve.wait_ge(bias_ready, g)
                dve.tensor_scalar(s_col[:, :], S_BANK[:, 0:T], score_b[:, mid:mid + 1], None, ALU.add).then_inc(s_ready, 1)
                if mid in PROJ:
                    dve.wait_ge(mask_made, proj_unit(g, mid) + 1)
                else:
                    dve.wait_ge(mask_in, 16 * (g - PAIRS + 1))
                if known(g):
                    dve.wait_ge(attn_ready, g)
                dve.sem_inc(taken, 1)
                for t in range(T):
                    last = dve.tensor_tensor_reduce(out=masked[:, t, :], in0=D_BANK[:, (t // KT) * N:(t // KT + 1) * N],
                                                    in1=adj_mask[:, t, :], scale=BIG, scalar=-3.0e38, op0=ALU.add,
                                                    op1=ALU.max, accum_out=row_max[:, t:t + 1])
                last.then_inc(max_ready, 1)
                dve.wait_ge(max_ready, g + 1)
                dve.wait_ge(s_ready, g + 1)
                dve.tensor_tensor(z_max[:, :], s_col[:, :], row_max[:, :], ALU.add).then_inc(z_ready, 1)
                dve.wait_ge(z_ready, g + 1)
                dve.scalar_tensor_tensor(out=m_col[:, :], in0=z_max[:, :], scalar=ALPHA[mid], in1=z_max[:, :],
                                         op0=ALU.mult, op1=ALU.max).then_inc(m_ready, 1)
                dve.wait_ge(m_ready, g + 1)
                if known(g):
                    dve.wait_ge(exps_done, g)
                dve.tensor_tensor(exp_bias[:, 0, :], s_col[:, :], m_col[:, :], ALU.subtract)
                dve.scalar_tensor_tensor(out=exp_bias[:, 1, :], in0=s_col[:, :], scalar=ALPHA[mid], in1=m_col[:, :],
                                         op0=ALU.mult, op1=ALU.subtract).then_inc(bias_ready, 1)

            def weights(g, mid):
                dve.wait_ge(exps_done, g + 1)
                if known(g):
                    dve.wait_ge(inv_ready, g)
                for t in range(T):
                    last = dve.scalar_tensor_tensor(out=attn[:, t, :], in0=attn[:, t, :], scalar=1.0, in1=masked[:, t, :],
                                                    op0=ALU.mult, op1=ALU.max, accum_out=row_sum[:, t:t + 1])
                last.then_inc(weights_made, 1)
                dve.wait_ge(weights_made, g + 1)
                if mid == TOPK:
                    n = 3 * (g - LAST)
                    dve.sem_inc(taken, 1)
                    for t in range(T):
                        last = dve.max(top_a[:, t, :], attn[:, t, :])
                    last.then_inc(top_step, 1)
                    dve.wait_ge(top_step, n + 1)
                    dve.sem_inc(taken, 1)
                    for t in range(T):
                        last = dve.match_replace(masked[:, t, :], top_a[:, t, :], attn[:, t, :], -1.0)
                    last.then_inc(top_step, 1)
                    dve.wait_ge(top_step, n + 2)
                    dve.sem_inc(taken, 1)
                    for t in range(T):
                        last = dve.max(top_b[:, t, :], masked[:, t, :])
                    last.then_inc(top_step, 1)
                    dve.wait_ge(top_step, n + 3)
                dve.reciprocal(inv_sum[:, :], row_sum[:, :]).then_inc(inv_ready, 1)
                if mid == TOPK:
                    for t in range(T):
                        last = dve.scalar_tensor_tensor(out=attn[:, t, :], in0=attn[:, t, :], scalar=top_b[:, t, 7:8],
                                                        in1=attn[:, t, :], op0=ALU.is_ge, op1=ALU.mult)
                    last.then_inc(attn_ready, 1)
                else:
                    dve.sem_inc(attn_ready, 1)

            def copy_attnT(g):
                dve.wait_ge(attn_turned, 2 * g + 2)
                if known(g):
                    dve.wait_ge(mixed, 2 * g)
                dve.tensor_copy(attnT[:, 1, :, :].rearrange("p a n -> p (a n)"), TR[1][:, :]).then_inc(attnT_d, 1)

            def elu_split(g, b):
                a = proj_unit(g, b)
                dve.wait_ge(inv_ready, g + 1)
                for t in range(T):
                    if t % 2 == 0:
                        dve.wait_ge(mixed, 2 * g + t // 2 + 1)
                    u = MIXB[t // 2][:, (t % 2) * D:(t % 2 + 1) * D]
                    dve.tensor_scalar(pos[:, t, :], u, inv_sum[:, t:t + 1], 0.0, ALU.mult, ALU.max)
                    last = dve.tensor_scalar(neg[:, t, :], u, inv_sum[:, t:t + 1], 0.0, ALU.mult, ALU.min)
                last.then_inc(elu_parts, 1)

            def residual(g, before, b):
                dve.wait_ge(xm_in, 16 * (g + 1))
                if before in FFN:
                    dve.wait_ge(res_scaled, g - FFN0)
                elif before is not None:
                    if before == BLOCKS - 1:
                        dve.wait_ge(out_saved, 16 * (g - LAST))
                    else:
                        dve.wait_ge(y_saved, 16 * (y_store(g - 1, before) + 1))
                    if before == 0:
                        dve.wait_ge(outer_saved, 16 * g)
                if b in PROJ:
                    a = proj_unit(g, b)
                    dve.wait_ge(elu_exp, a + 1)
                    dve.scalar_tensor_tensor(out=y[:, :, :], in0=neg[:, :, :], scalar=-1.0, in1=pos[:, :, :],
                                             op0=ALU.add, op1=ALU.add).then_inc(elu_sum, 1)
                    dve.wait_ge(elu_sum, a + 1)
                    dve.tensor_tensor(y[:, :, :], y[:, :, :], x_mix[:, :, :], ALU.add).then_inc(y_ready, 1)
                else:
                    dve.wait_ge(inv_ready, g + 1)
                    for t in range(T):
                        if t % 2 == 0:
                            dve.wait_ge(mixed, 2 * g + t // 2 + 1)
                        last = dve.scalar_tensor_tensor(out=y[:, t, :], in0=MIXB[t // 2][:, (t % 2) * D:(t % 2 + 1) * D],
                                                        scalar=inv_sum[:, t:t + 1], in1=x_mix[:, t, :],
                                                        op0=ALU.mult, op1=ALU.add)
                    last.then_inc(y_ready, 1)
                dve.wait_ge(y_ready, g + 1)
                layer_norm(0, g, y)

            def split_h(g):
                f = g - FFN0
                dve.wait_ge(hT_ready, 2 * f + 2)
                if known(f):
                    dve.wait_ge(hid_done, FT * f)
                dve.tensor_copy(h_hi[:, :, :], hT).then_inc(h_hi_ready, 1)
                dve.wait_ge(h_hi_ready, f + 1)
                dve.tensor_tensor(h_lo[:, :, :], hT, h_hi[:, :, :].bitcast(F32), ALU.subtract).then_inc(h_ready, 1)

            def split_act(k, ft):
                f = k - FFN0
                dve.wait_ge(act_ready, FT * f + ft + 1)
                if ft >= 4 or known(f):
                    dve.wait_ge(ff_done, FT * f + ft - 3)
                dve.tensor_copy(act_hi[:, ft % 4, :], act[:, ft % 2, :]).then_inc(act_hi_ready, 1)
                dve.wait_ge(act_hi_ready, FT * f + ft + 1)
                dve.tensor_tensor(act_lo[:, ft % 4, :], act[:, ft % 2, :], act_hi[:, ft % 4, :].bitcast(F32),
                                  ALU.subtract).then_inc(act_split, 1)

            def step(k, prev, cur, mid, front):
                if isinstance(k, int) and k % PAIRS == PAIRS - 2 and 0 < k and k // PAIRS + 1 in range(2, BLOCKS):
                    prepare(k // PAIRS + 1)
                if mid is not None:
                    scores(k + 1, cur, mid)
                f1 = k - 1 - FFN0
                if prev in FFN:
                    dve.wait_ge(ff_done, FT * (f1 + 1))
                    dve.wait_ge(res_ready, f1 + 1)
                    if known(f1):
                        dve.wait_ge(y2_saved, 16 * f1)
                    for c in range(2):
                        last = dve.tensor_tensor(y2[:, 2 * c:2 * c + 2, :].rearrange("p a n -> p (a n)"), ACC[c][:, :],
                                                 h_res[:, 2 * c:2 * c + 2, :].rearrange("p a n -> p (a n)"), ALU.add)
                    last.then_inc(y2_ready, 1)
                if cur in FFN:
                    split_act(k, 0)
                    split_act(k, 1)
                if prev in FFN:
                    dve.wait_ge(y2_ready, f1 + 1)
                    layer_norm(1, f1, y2)
                if cur in FFN:
                    split_act(k, 2)
                    split_act(k, 3)
                if prev in FFN:
                    finish(1, f1, y2)
                if cur in PROJ:
                    elu_split(k, cur)
                elif cur is not None and cur not in FFN:
                    residual(k, prev, cur)
                if mid is not None:
                    weights(k + 1, mid)
                if cur in PROJ:
                    residual(k, prev, cur)
                if cur in FFN:
                    split_act(k, 4)
                if mid is not None:
                    copy_attnT(k + 1)
                if cur in FFN:
                    for ft in range(5, FT):
                        split_act(k, ft)
                elif cur is not None:
                    finish(0, k, y)
                if mid in FFN:
                    residual(k + 1, cur, mid)
                    finish(0, k + 1, y)
                    split_h(k + 1)
                if prev == FFN[-1]:
                    n = k - 1 - prev * PAIRS
                    dve.wait_ge(outer_added, n + 1)
                    layer_norm(2, n, y2)
                    finish(2, n, y2)

            drive(dve, step)

        @block.tensor
        def _(pe):
            pe.wait_ge(ident_ready, 2)
            pe.wait_ge(consts_in, 16 * (8 + 5 * LAYERS))
            pe.transpose(TR[0][:, 0:V_ROWS], vec_rows[:, :], ident[0:V_ROWS, 0:V_ROWS]).then_inc(vec_mm, 1)
            pe.wait_ge(vec_ready, 1)

            def hidden(k, ft):
                f = k - FFN0
                if ft >= 4:
                    pe.wait_ge(act_ready, FT * f + ft - 3)
                if ft == 2:
                    pe.wait_ge(s_ready, k + 2)
                if ft == 3:
                    pe.wait_ge(max_ready, k + 2)
                o = HID[ft % 4][:, :]
                for c in range(KT):
                    col = slice(ft * P, (ft + 1) * P)
                    pe.matmul(o, w1_hi[:, c, col], h_hi[:, c, :], start=(c == 0), stop=False)
                    pe.matmul(o, w1_hi[:, c, col], h_lo[:, c, :], start=False, stop=False)
                    last = pe.matmul(o, w1_lo[:, c, col], h_hi[:, c, :], start=False, stop=(c == KT - 1))
                last.then_inc(hid_done, 1)

            def down(k, ft):
                f = k - FFN0
                pe.wait_ge(act_split, FT * f + ft + 1)
                if ft == 0 and known(f):
                    pe.wait_ge(y2_ready, f)
                for t in range(T):
                    o = ACC[t // 2][:, (t % 2) * D:(t % 2 + 1) * D]
                    col = slice(t * P, (t + 1) * P)
                    pe.matmul(o, act_hi[:, ft % 4, col], w2_hi[:, ft, :], start=(ft == 0 and t % 2 == 0), stop=False,
                              skip_group_check=True)
                    pe.matmul(o, act_hi[:, ft % 4, col], w2_lo[:, ft, :], start=False, stop=False, skip_group_check=True)
                    last = pe.matmul(o, act_lo[:, ft % 4, col], w2_hi[:, ft, :], start=False, stop=(ft == FT - 1),
                                     skip_group_check=True)
                last.then_inc(ff_done, 1)

            def turn_attn(g):
                pe.wait_ge(attn_ready, g + 1)
                for u in range(2):
                    for j in range(KT):
                        for i in range(KT):
                            last = pe.transpose(TR[u][:, (j * KT + i) * P:(j * KT + i + 1) * P],
                                                attn[:, u * KT + i, j * P:(j + 1) * P], ident[:, :])
                    last.then_inc(attn_turned, 1)

            def mix(k, g, cur, mid):
                if mid in PROJ:
                    pe.wait_ge(values_ready, 2 * (proj_unit(g, mid) + 1))
                else:
                    pe.wait_ge(xm_in, 16 * (g + 1))
                if cur in FFN:
                    pe.wait_ge(act_ready, FT * (k - FFN0) + 6)
                elif cur in PROJ:
                    pe.wait_ge(elu_parts, proj_unit(k, cur) + 1)
                elif cur is not None:
                    pe.wait_ge(y_ready, g)
                v = values if mid in PROJ else x_mix
                for u in range(2):
                    pe.wait_ge(attnT_a if u == 0 else attnT_d, g + 1)
                    for i in range(KT):
                        for j in range(KT):
                            last = pe.matmul(MIXB[u][:, i * D:(i + 1) * D], attnT[:, u, j, i * P:(i + 1) * P],
                                             v[:, u * KT + j, :], start=(j == 0), stop=(j == KT - 1))
                    last.then_inc(mixed, 1)

            def turn_x(g):
                pe.wait_ge(xs_in, 16 * (g + 1))
                for u in range(KT):
                    for t in range(T):
                        last = pe.transpose(TR[u][:, t * P:(t + 1) * P], x_front[:, t, u * P:(u + 1) * P], ident[:, :])
                    last.then_inc(x_turned, 1)

            def score(k, g, cur, front):
                pe.wait_ge(xT_ready, 2 * g + 2)
                if isinstance(g, int) and g % PAIRS == 0:
                    pe.wait_ge(prep_ready, g // PAIRS + 1)
                if cur in FFN:
                    pe.wait_ge(act_ready, FT * (k - FFN0) + FT)
                elif known(g):
                    pe.wait_ge(max_ready, g)
                    pe.wait_ge(s_ready, g)
                for c in range(KT):
                    pe.matmul(D_BANK[:, :], dst_rep[:, front % 2, c, :], xT[:, c, :], start=(c == 0), stop=(c == KT - 1))
                for t in range(T):
                    for c in range(KT):
                        last = pe.matmul(S_BANK[:, t:t + 1], xT[:, c, t * P:(t + 1) * P], columns(front, 0)[:, c:c + 1],
                                         start=(c == 0), stop=(c == KT - 1))
                last.then_inc(scored, 1)
                if front in PROJ:
                    a = proj_unit(g, front)
                    if known(a):
                        pe.wait_ge(values_ready, 2 * a)
                    if front == TOPK and isinstance(g, int):
                        pe.wait_ge(y2_ready, 3 * PAIRS)
                    for t in range(T):
                        for c in range(KT):
                            last = pe.matmul(ACC[t // 2][:, (t % 2) * D:(t % 2 + 1) * D], xT[:, c, t * P:(t + 1) * P],
                                             w_proj[:, c, :], start=(c == 0), stop=(c == KT - 1))
                    last.then_inc(projected, 1)

            def step(k, prev, cur, mid, front):
                g, g2 = k + 1, k + 2
                if cur in FFN:
                    if isinstance(k, int) and k % PAIRS == 0:
                        if cur == FFN[0]:
                            pe.wait_ge(chunk_split, 4 * LAYERS)
                        else:
                            pe.wait_ge(w1_in, 16 * 2 * (cur - 1))
                    pe.wait_ge(h_ready, k - FFN0 + 1)
                    for ft in range(4):
                        hidden(k, ft)
                    for ft in range(4):
                        if ft == 3:
                            turn_attn(g)
                        hidden(k, ft + 4)
                        if ft == 0 and isinstance(k, int) and k % PAIRS == 0 and cur != FFN[0]:
                            pe.wait_ge(w2_in, 16 * 2 * (cur - 1))
                        down(k, ft)
                    mix(k, g, cur, mid)
                    down(k, 4)
                    down(k, 5)
                    turn_x(g2)
                    down(k, 6)
                    down(k, 7)
                else:
                    if front is not None:
                        turn_x(g2)
                        score(k, g2, cur, front)
                    if mid is not None:
                        turn_attn(g)
                        mix(k, g, cur, mid)
                if mid in FFN:
                    pe.wait_ge(normed[0], g + 1)
                    if cur in FFN:
                        pe.wait_ge(xT_ready, 2 * g2 + 2)
                    for u in range(KT):
                        for t in range(T):
                            last = pe.transpose(TR[u][:, t * P:(t + 1) * P], y[:, t, u * P:(u + 1) * P], ident[:, :])
                        last.then_inc(n_turned, 1)
                if cur in FFN:
                    score(k, g2, cur, front)

            drive(pe, step)


_INS = ['x', 'adj', 'L0_gnn_w', 'L0_gnn_a1', 'L0_gnn_a2', 'L1_gnn_attn_w', 'L1_gnn_attn_b', 'L1_gnn_W1', 'L1_gnn_b1',
        'L1_gnn_W2', 'L1_gnn_b2', 'L1_gnn_g1', 'L1_gnn_beta1', 'L1_gnn_g2', 'L1_gnn_beta2', 'L2_gnn_attn_w_src',
        'L2_gnn_attn_w_dst', 'L2_gnn_attn_b', 'L3_gnn_W', 'L3_gnn_a']
_OUTS = [((GRAPHS, N, D), 'float32')]


def kernel(**inputs):
    import numpy as _np
    import concourse.bacc as _bacc
    from concourse import mybir as _mybir
    from concourse.bass_utils import run_bass_kernel_spmd as _run

    nc = _bacc.Bacc("TRN2", target_bir_lowering=False, num_devices=1)
    arrays, args = {}, []
    for name in _INS:
        a = _np.ascontiguousarray(inputs[name])
        arrays[f"in_{name}_dram"] = a
        args.append(nc.dram_tensor(f"in_{name}_dram", a.shape, _mybir.dt.from_np(a.dtype), kind="ExternalInput").ap())
    for i, (shape, dtype) in enumerate(_OUTS):
        dt = _mybir.dt.from_np(_np.dtype(dtype))
        args.append(nc.dram_tensor(f"out_{i}_dram", shape, dt, kind="ExternalOutput").ap())
    graph_stack(nc, *args)
    r = _run(nc, [arrays], core_ids=[0])
    got = tuple(r.results[0][f"out_{i}_dram"] for i in range(len(_OUTS)))
    return got[0]
```

```python
import concourse.bass as bass
from concourse import mybir
from contextlib import ExitStack

F32 = mybir.dt.float32
F32R = mybir.dt.float32r
I32 = mybir.dt.int32
I8 = mybir.dt.int8
ALU = mybir.AluOpType
ACT = mybir.ActivationFunctionType

P = 128
GRAPHS, N, D = 32, 256, 256
PAIRS = GRAPHS // 2
T = 2 * N // P
KT = D // P
TOK = 2 * N
LAYERS, FF = 3, 1024
FT = FF // P
BLOCKS = 6
UNITS = BLOCKS * PAIRS
FFN = (1, 2, 3)
PROJ = (0, 5)
TOPK = 5
ROW_S = (1, 2)
ROW_FIRST = PAIRS + 2
ROW_LAST = 3 * PAIRS - 1
AVG_FIRST = 4 * PAIRS + 2
ALPHA = (0.1, 0.2, 0.2, 0.2, 0.2, 0.2)
EPS = 1e-5
BIG = 2.0 ** 64
FFN0 = FFN[0] * PAIRS
LAST = UNITS - PAIRS

CONSTS = 13
V_ATT, V_B1, V_G1, V_BETA1, V_SRC, V_DST, V_ROWS = 0, 12, 36, 42, 48, 50, 52


def graph_stack(nc, x, adj, w0, a0_src, a0_dst, attn_w, attn_b, w1, b1, w2, b2, g1, beta1, g2, beta2,
                l2_src, l2_dst, l2_b, w3, a3, out):
    x_t = x.rearrange("b (i p) d -> p (b i) d", p=P)
    adj_t = adj.rearrange("b (i p) j -> p (b i) j", p=P)
    out_t = out.rearrange("b (i p) d -> p (b i) d", p=P)
    x_outer = nc.dram_tensor("x_outer", (P, PAIRS * T, D), F32, kind="Internal").ap()

    ctx = ExitStack()
    with ctx:
        def sb(name, shape, dt=F32):
            return ctx.enter_context(nc.sbuf_tensor(name, shape, dt))

        def sem(name):
            return ctx.enter_context(nc.semaphore(name))

        state = sb("state", [P, PAIRS * T, D])
        edges = sb("edges", [P, PAIRS * T, N], I8)
        w1_hi = sb("w1_hi", [P, KT, FF], F32R)
        w1_lo = sb("w1_lo", [P, KT, FF], F32R)
        w2_hi = sb("w2_hi", [P, FT, D], F32R)
        w2_lo = sb("w2_lo", [P, FT, D], F32R)
        w_proj = sb("w_proj", [P, KT, D])
        a_rows = sb("a_rows", [P, 2, D])
        wa = sb("wa", [P, 2, 2, KT])
        dst_rep = sb("dst_rep", [P, 2, KT, P])
        vec_rows = sb("vec_rows", [V_ROWS, P])
        vec = sb("vec", [P, V_ROWS])
        score_b = sb("score_b", [P, BLOCKS])
        norm_w = sb("norm_w", [P, LAYERS, 4, D])
        ident = sb("ident", [P, P])
        neg_half = sb("neg_half", [P, T])
        x_front = sb("x_front", [P, T, D])
        x_mix = sb("x_mix", [P, T, D])
        xT = sb("xT", [P, KT, TOK])
        adj_mask = sb("adj_mask", [P, T, N], I8)
        loop_mask = sb("loop_mask", [P, T, N], I8)
        masked = sb("masked", [P, T, N])
        attn = sb("attn", [P, T, N])
        attnT = sb("attnT", [P, 2, KT, N])
        y = sb("y", [P, T, D])
        values = sb("values", [P, T, D])
        h_hi = sb("h_hi", [P, KT, TOK], F32R)
        h_lo = sb("h_lo", [P, KT, TOK], F32R)
        h_res = sb("h_res", [P, T, D])
        act = sb("act", [P, 2, TOK])
        act_hi = sb("act_hi", [P, 4, TOK], F32R)
        act_lo = sb("act_lo", [P, 4, TOK], F32R)
        y2 = sb("y2", [P, T, D])
        s_sum = sb("s_sum", [P, T])
        s_col = sb("s_col", [P, T])
        row_max = sb("row_max", [P, T])
        z_max = sb("z_max", [P, T])
        m_col = sb("m_col", [P, T])
        exp_bias = sb("exp_bias", [P, 2, T])
        row_sum = sb("row_sum", [P, T])
        inv_sum = sb("inv_sum", [P, T])
        inv_late = sb("inv_late", [P, T])
        top_a = sb("top_a", [P, T, 8])
        top_b = sb("top_b", [P, T, 8])
        stats = [sb(f"stats{i}", [P, T, 6]) for i in range(3)]
        mean_var = [sb(f"mean_var{i}", [P, T, 2]) for i in range(3)]
        var_eps = [sb(f"var_eps{i}", [P, T]) for i in range(3)]
        rstd = [sb(f"rstd{i}", [P, T]) for i in range(3)]

        adj_in = act[:, :, :].bitcast(I32).rearrange("p a (t j) -> p (a t) j", j=N)
        hT = attn[:, :, :].rearrange("p (u a) n -> p u (a n)", u=KT)
        x_saved = values
        elu_e = y2
        elu_r = h_res
        normed_avg = h_res

        bank = [ctx.enter_context(nc.psum_tensor(f"bank{i}", [P, 512], F32)) for i in range(8)]
        TR = bank[0:2]
        ACC = bank[2:4]
        HID = bank[4:8]
        MIXB, S_BANK, D_BANK = HID[0:2], HID[2], HID[3]

        consts_in = sem("consts_in")
        wproj_in = sem("wproj_in")
        chunk_in = [sem(f"chunk_in{i}") for i in range(2)]
        chunk_split = sem("chunk_split")
        chunk_part = sem("chunk_part")
        ident_ready = sem("ident_ready")
        vec_mm = sem("vec_mm")
        vec_ready = sem("vec_ready")
        wa_ready = sem("wa_ready")
        src_in = sem("src_in")
        prep_ready = sem("prep_ready")
        bb_ready = sem("bb_ready")
        xs_in = sem("xs_in")
        xm_in = sem("xm_in")
        av_in = sem("av_in")
        mask_in = sem("mask_in")
        adj_loaded = sem("adj_loaded")
        mask_made = sem("mask_made")
        loops_made = sem("loops_made")
        edges_saved = sem("edges_saved")
        y_saved = sem("y_saved")
        y2_saved = sem("y2_saved")
        outer_saved = sem("outer_saved")
        saved_in = sem("saved_in")
        out_saved = sem("out_saved")
        x_turned = sem("x_turned")
        xT_ready = sem("xT_ready")
        scored = sem("scored")
        s_scored = sem("s_scored")
        projected = sem("projected")
        values_ready = sem("values_ready")
        s_summed = sem("s_summed")
        s_ready = sem("s_ready")
        max_ready = sem("max_ready")
        z_ready = sem("z_ready")
        m_ready = sem("m_ready")
        bias_ready = sem("bias_ready")
        exps_done = sem("exps_done")
        weights_made = sem("weights_made")
        inv_ready = sem("inv_ready")
        top_step = sem("top_step")
        attn_ready = sem("attn_ready")
        attn_turned = sem("attn_turned")
        attnT_a = sem("attnT_a")
        attnT_d = sem("attnT_d")
        mixed = sem("mixed")
        inv_kept = sem("inv_kept")
        elu_pos = sem("elu_pos")
        elu_exp = sem("elu_exp")
        elu_sum = sem("elu_sum")
        y_ready = sem("y_ready")
        stats_done = [sem(f"stats_done{i}") for i in range(3)]
        moments = [sem(f"moments{i}") for i in range(3)]
        var_ready = [sem(f"var_ready{i}") for i in range(3)]
        rstd_ready = [sem(f"rstd_ready{i}") for i in range(3)]
        normed = [sem(f"normed{i}") for i in range(3)]
        n_turned = sem("n_turned")
        hT_ready = sem("hT_ready")
        h_hi_ready = sem("h_hi_ready")
        h_ready = sem("h_ready")
        res_scaled = sem("res_scaled")
        res_ready = sem("res_ready")
        hid_done = sem("hid_done")
        act_ready = sem("act_ready")
        act_hi_ready = sem("act_hi_ready")
        act_split = sem("act_split")
        ff_done = sem("ff_done")
        y2_ready = sem("y2_ready")
        x_scaled = sem("x_scaled")
        x_ready = sem("x_ready")
        outer_added = sem("outer_added")
        taken = sem("taken")

        block = ctx.enter_context(nc.Block())

        def rows(pair):
            return bass.ds(pair * T, T)

        def words(w):
            return w[:, :, :].rearrange("p k f -> p (k f)").bitcast(F32)

        def columns(b, which):
            if b in PROJ:
                return wa[:, PROJ.index(b), which, :]
            if b in FFN:
                c = V_ATT + ((b - 1) * 2 + which) * KT
                return vec[:, c:c + KT]
            c = V_DST if which else V_SRC
            return vec[:, c:c + KT]

        def proj_unit(g, b):
            return g if b == 0 else g - LAST + PAIRS

        def by_rows(g, b):
            return ROW_FIRST <= g <= ROW_LAST if isinstance(g, int) else b in ROW_S

        def s_unit(g, b):
            low = g < ROW_FIRST if isinstance(g, int) else b == 0
            return g if low else g - (ROW_LAST - ROW_FIRST + 1)

        def own_values(g, b):
            return b == 4 and (not isinstance(g, int) or g >= AVG_FIRST)

        def block_of(g, near):
            return near if not isinstance(g, int) else int(g // PAIRS) if 0 <= g < UNITS else None

        def y_store(g, b):
            return g - {0: 0, 4: 3 * PAIRS, 5: 3 * PAIRS}[b]

        def drive(eng, step):
            def of(g):
                return int(g // PAIRS) if 0 <= g < UNITS else None

            def straight(k):
                step(k, of(k - 1), of(k), of(k + 1), of(k + 2))

            for k in (-2, -1):
                straight(k)
            for b in range(BLOCKS):
                first = 3 if b == 0 else 1
                for p in range(first):
                    straight(b * PAIRS + p)
                with eng.Fori(first, PAIRS - 4) as p:
                    step(p + b * PAIRS, b, b, b, b)
                for p in range(PAIRS - 4, PAIRS):
                    straight(b * PAIRS + p)

        def k_is(k, n):
            return isinstance(k, int) and k == n

        def known(g, least=1):
            return not isinstance(g, int) or g >= least

        @block.sync
        def _(sp):
            ld = nc.allow_non_contiguous_dma(reason="small constants")
            ld.__enter__()
            sp.dma_start(x_front[:, :, :], x_t[:, 0:T, :]).then_inc(xs_in, 16)
            sp.dma_start(w_proj[:, :, :], w0.rearrange("(t p) n -> p t n", p=P)).then_inc(wproj_in, 16)
            for i, src in enumerate((a0_src, a0_dst)):
                sp.dma_start(a_rows[:, i, :], src.rearrange("n o -> o n").to_broadcast([P, D])).then_inc(wproj_in, 16)

            def load_constants():
                for base, src in ((V_ATT, attn_w.rearrange("l (r q) -> (l r) q", q=P)),
                                  (V_B1, b1.rearrange("l (r q) -> (l r) q", q=P)),
                                  (V_G1, g1.rearrange("l (r q) -> (l r) q", q=P)),
                                  (V_BETA1, beta1.rearrange("l (r q) -> (l r) q", q=P)),
                                  (V_SRC, l2_src.rearrange("(r q) -> r q", q=P)),
                                  (V_DST, l2_dst.rearrange("(r q) -> r q", q=P))):
                    sp.dma_start(vec_rows[base:base + src.shape[0], :], src).then_inc(consts_in, 16)
                sp.dma_start(score_b[:, 1:4], attn_b.unsqueeze(0).to_broadcast([P, LAYERS])).then_inc(consts_in, 16)
                sp.dma_start(score_b[:, 4:5], l2_b.unsqueeze(0).to_broadcast([P, 1])).then_inc(consts_in, 16)
                for i, src in enumerate((g1, beta1, g2, beta2)):
                    sp.dma_start(norm_w[:, :, i, :], src.unsqueeze(0).to_broadcast([P, LAYERS, D])).then_inc(consts_in, 16)
                sp.dma_start(y[:, 0:LAYERS, :], b2.unsqueeze(0).to_broadcast([P, LAYERS, D])).then_inc(consts_in, 16)
                sp.wait_ge(wa_ready, 1)
                for l in range(len(ROW_S)):
                    sp.dma_start(a_rows[:, l, :], attn_w[l:l + 1, 0:D].to_broadcast([P, D])).then_inc(src_in, 16)

            def load_quarter(l, q, raw, n):
                if q < 2:
                    sp.dma_start(raw[:, :, :].rearrange("p t n -> p (t n)"), w1[l, q * P:(q + 1) * P, :])\
                        .then_inc(chunk_in[n], 16)
                else:
                    src = w2[l, (q - 2) * 4 * P:(q - 1) * 4 * P, :].rearrange("(t p) n -> p t n", p=P)
                    sp.dma_start(raw[:, :, :], src).then_inc(chunk_in[n], 16)

            def load_mask(g, b):
                if known(g):
                    sp.wait_ge(max_ready, g)
                if b == 1 and isinstance(g, int):
                    sp.wait_ge(loops_made, min(g, PAIRS))
                sp.wait_ge(edges_saved, 16 * (g - b * PAIRS + 1))
                sp.sem_inc(taken, 1)
                sp.dma_start(adj_mask[:, :, :], edges[:, rows(g - b * PAIRS), :]).then_inc(mask_in, 16)

            def load_adj(g, b):
                a = proj_unit(g, b)
                if known(a):
                    sp.wait_ge(mask_made, a)
                if b == TOPK and isinstance(g, int):
                    sp.wait_ge(act_split, FT * 3 * PAIRS)
                sp.sem_inc(taken, 1)
                sp.dma_start(adj_in, adj_t[:, rows(g - b * PAIRS), :]).then_inc(adj_loaded, 16)

            def load_x(g, b, dst, done):
                if b - 1 in FFN:
                    sp.wait_ge(y2_saved, (g - PAIRS - FFN0 + 1) * 16)
                elif b > 0:
                    sp.wait_ge(y_saved, (y_store(g - PAIRS, b - 1) + 1) * 16)
                sp.sem_inc(taken, 1)
                src = x_t if b == 0 else state
                sp.dma_start(dst[:, :, :], src[:, rows(g - b * PAIRS), :]).then_inc(done, 16)

            def load_front(g, near):
                if isinstance(g, int) and g >= UNITS:
                    return
                sp.wait_ge(x_turned, 2 * g)
                sp.sem_inc(taken, 1)
                if by_rows(g - 1, near):
                    sp.wait_ge(s_summed, g - ROW_FIRST)
                    sp.sem_inc(taken, 1)
                load_x(g, block_of(g, near), x_front, xs_in)

            def save_layer(g, b):
                if b == FFN[-1]:
                    sp.wait_ge(normed[2], g - b * PAIRS + 1)
                else:
                    sp.wait_ge(x_ready, g - FFN0 + 1)
                sp.sem_inc(taken, 1)
                sp.dma_start(state[:, rows(g - b * PAIRS), :], y2[:, :, :]).then_inc(y2_saved, 16)

            def load_edges(g, near):
                b = block_of(g, near)
                if b in PROJ:
                    load_adj(g, b)
                elif b is not None:
                    load_mask(g, b)

            def step(k, prev, cur, mid, front):
                if k_is(k, -2):
                    load_edges(0, 0)
                    load_front(1, 0)
                if cur in FFN and k_is(k, cur * PAIRS) and cur != FFN[0]:
                    sp.wait_ge(chunk_split, 4 * (cur - 1) + 3)
                    load_quarter(cur - 1, 3, values, 0)
                if own_values(k + 1, mid):
                    sp.wait_ge(mixed, 2 * (k + 1))
                    sp.sem_inc(taken, 1)
                    if k_is(k, AVG_FIRST - 1):
                        sp.wait_ge(outer_added, PAIRS)
                        sp.sem_inc(taken, 1)
                    sp.dma_start(values[:, :, :], state[:, rows(k + 1 - mid * PAIRS), :]).then_inc(av_in, 16)
                if mid in FFN and front is not None:
                    load_edges(k + 2, front)
                if prev in FFN and cur in FFN:
                    save_layer(k - 1, prev)

                if cur == FFN[-1]:
                    if known(k, FFN[-1] * PAIRS + 1):
                        sp.wait_ge(outer_added, k - FFN[-1] * PAIRS)
                    else:
                        sp.wait_ge(outer_saved, 16 * PAIRS)
                    if k_is(k, FFN[-1] * PAIRS):
                        sp.wait_ge(chunk_split, 4 * LAYERS)
                    sp.sem_inc(taken, 1)
                    sp.dma_start(x_saved[:, :, :], x_outer[:, rows(k - cur * PAIRS), :]).then_inc(saved_in, 16)
                next_layer = cur in FFN and mid in FFN and k_is(k, cur * PAIRS + PAIRS - 1)
                if next_layer:
                    sp.wait_ge(chunk_split, 4 * cur + 1)
                    load_quarter(cur, 1, values, 0)
                if k_is(k, 3 * PAIRS):
                    sp.wait_ge(projected, PAIRS)
                    sp.wait_ge(s_summed, ROW_LAST - ROW_FIRST + 1)
                    sp.dma_start(w_proj[:, :, :], w3.rearrange("(t p) n -> p t n", p=P)).then_inc(wproj_in, 16)
                    sp.dma_start(a_rows[:, :, :], a3.rearrange("(h n) o -> o h n", h=2).to_broadcast([P, 2, D]))\
                      .then_inc(wproj_in, 16)
                if cur not in FFN and mid is not None:
                    if cur in PROJ:
                        sp.wait_ge(elu_sum, proj_unit(k, cur) + 1)
                    elif cur is not None:
                        sp.wait_ge(y_ready, k + 1)
                    sp.sem_inc(taken, 1)
                    load_x(k + 1, mid, x_mix, xm_in)
                if front == 0:
                    sp.wait_ge(loops_made, k + 3)
                    sp.sem_inc(taken, 1)
                    sp.dma_start(edges[:, rows(k + 2), :], loop_mask[:, :, :]).then_inc(edges_saved, 16)
                if cur not in FFN and front not in FFN and front is not None:
                    load_edges(k + 3, front)
                if cur not in FFN and mid not in FFN:
                    load_front(k + 4, front)
                if cur is not None and cur not in FFN:
                    sp.wait_ge(normed[0], k + 1)
                    sp.sem_inc(taken, 1)
                    where = rows(k - cur * PAIRS)
                    src = normed_avg if cur == 4 else values if k_is(k, PAIRS - 1) else y
                    if cur == BLOCKS - 1:
                        sp.dma_start(out_t[:, where, :], src[:, :, :]).then_inc(out_saved, 16)
                    else:
                        sp.dma_start(state[:, where, :], src[:, :, :]).then_inc(y_saved, 16)
                    if cur == 0:
                        sp.dma_start(x_outer[:, where, :], src[:, :, :]).then_inc(outer_saved, 16)
                if prev in FFN and cur not in FFN:
                    save_layer(k - 1, prev)
                if mid in FFN and front is not None:
                    sp.wait_ge(y_ready, k + 2)
                    load_x(k + 2, front, x_mix, xm_in)
                if cur in FFN:
                    load_front(k + 3, front)
                    if mid not in FFN:
                        load_front(k + 4, front)
                    if front not in FFN:
                        load_edges(k + 3, front)
                if k_is(k, -2):
                    load_constants()
                    load_quarter(0, 0, h_res, 0)
                    load_quarter(0, 1, y2, 1)
                if k_is(k, -1):
                    sp.wait_ge(chunk_split, 1)
                    load_quarter(0, 2, h_res, 0)
                    sp.wait_ge(chunk_split, 2)
                    load_quarter(0, 3, y2, 1)
                if cur in FFN and cur != FFN[-1] and k_is(k, cur * PAIRS + PAIRS - 2):
                    sp.wait_ge(chunk_split, 4 * cur)
                    load_quarter(cur, 0, values, 0)
                if next_layer:
                    sp.wait_ge(chunk_split, 4 * cur + 2)
                    load_quarter(cur, 2, values, 0)

            drive(sp, step)
            ld.__exit__(None, None, None)
            sp.wait_ge(out_saved, 16 * PAIRS)
            sp.wait_ge(outer_saved, 16 * PAIRS)

        @block.gpsimd
        def _(pool):
            pool.memset(neg_half[:, :], -0.5)
            pool.memset(ident[:, :], 0.0).then_inc(ident_ready, 1)
            pool.wait_ge(ident_ready, 1)
            pool.affine_select(out=ident[:, :], in_=ident[:, :], compare_op=ALU.not_equal, fill=1.0, base=0,
                               pattern=[[-1, P]], channel_multiplier=1).then_inc(ident_ready, 1)
            pool.wait_ge(ident_ready, 2)

            def rsqrt(i, n):
                pool.wait_ge(var_ready[i], n + 1)
                pool.tensor_tensor(rstd[i][:, :], var_eps[i][:, :], neg_half[:, :], ALU.pow).then_inc(rstd_ready[i], 1)

            def wide(l, i):
                return norm_w[:, l:l + 1, i, :].to_broadcast([P, T, D])

            def step(k, prev, cur, mid, front):
                if front == 0:
                    g = k + 2
                    pool.wait_ge(mask_made, g + 1)
                    if known(g):
                        pool.wait_ge(edges_saved, 16 * g)
                    pool.sem_inc(taken, 1)
                    pool.affine_select(out=loop_mask[:, :, :].rearrange("p (b i) j -> p b i j", b=2),
                                       in_=adj_mask[:, :, :].rearrange("p (b i) j -> p b i j", b=2),
                                       compare_op=ALU.not_equal, fill=0.0, base=0,
                                       pattern=[[0, 2], [P, KT], [-1, N]], channel_multiplier=1)\
                        .then_inc(loops_made, 1)
                if k_is(k, -1):
                    pool.wait_ge(consts_in, 16 * CONSTS)
                    pool.tensor_tensor(norm_w[:, :, 1, :], norm_w[:, :, 1, :], y[:, 0:LAYERS, :], ALU.add)\
                        .then_inc(bb_ready, 1)
                if prev in FFN:
                    rsqrt(1, k - 1 - FFN0)
                if cur in FFN:
                    f = k - FFN0
                    pool.wait_ge(normed[0], k + 1)
                    if known(f):
                        pool.wait_ge(y2_ready, f)
                    pool.tensor_tensor(h_res[:, :, :], y[:, :, :], wide(cur - 1, 0), ALU.mult).then_inc(res_scaled, 1)
                if prev in FFN:
                    f = k - 1 - FFN0
                    pool.wait_ge(normed[1], f + 1)
                    pool.tensor_tensor(y2[:, :, :], y2[:, :, :], wide(prev - 1, 2), ALU.mult).then_inc(x_scaled, 1)
                    pool.wait_ge(x_scaled, f + 1)
                    pool.tensor_tensor(y2[:, :, :], y2[:, :, :], wide(prev - 1, 3), ALU.add).then_inc(x_ready, 1)
                    if prev == FFN[-1]:
                        n = k - 1 - prev * PAIRS
                        pool.wait_ge(x_ready, f + 1)
                        pool.wait_ge(saved_in, 16 * (n + 1))
                        pool.tensor_tensor(y2[:, :, :], y2[:, :, :], x_saved[:, :, :], ALU.add).then_inc(outer_added, 1)
                if cur is not None and cur not in FFN:
                    rsqrt(0, k)
                if mid in FFN:
                    rsqrt(0, k + 1)
                if cur in FFN:
                    f = k - FFN0
                    pool.wait_ge(res_scaled, f + 1)
                    pool.tensor_tensor(h_res[:, :, :], h_res[:, :, :], wide(cur - 1, 1), ALU.add).then_inc(res_ready, 1)
                if prev == FFN[-1]:
                    rsqrt(2, k - 1 - prev * PAIRS)

            drive(pool, step)

        @block.scalar
        def _(act_e):

            def gelu(k, cur, ft):
                f = k - FFN0
                act_e.wait_ge(hid_done, FT * f + ft + 1)
                if ft >= 2 or known(f):
                    act_e.wait_ge(act_split, FT * f + ft - 1)
                c = V_B1 + (cur - 1) * FT + ft
                act_e.activation(act[:, ft % 2, :], HID[ft % 4][:, :], ACT.Gelu, bias=vec[:, c:c + 1])\
                    .then_inc(act_ready, 1)

            def exps_steep(g, before):
                act_e.wait_ge(bias_ready, g + 1)
                if before in FFN:
                    act_e.wait_ge(h_ready, 2 * (g - FFN0))
                elif known(g):
                    act_e.wait_ge(attn_turned, 2 * g)
                for t in range(T):
                    act_e.activation(attn[:, t, :], masked[:, t, :], ACT.Exp, bias=exp_bias[:, 0, t:t + 1])

            def exps_flat(g, mid):
                for t in range(T):
                    last = act_e.activation(masked[:, t, :], masked[:, t, :], ACT.Exp,
                                            bias=exp_bias[:, 1, t:t + 1], scale=ALPHA[mid])
                last.then_inc(exps_done, 1)

            def elu_part(dst, func, done):
                for t in range(T):
                    last = act_e.activation(dst[:, t, :], MIXB[t // 2][:, (t % 2) * D:(t % 2 + 1) * D], func,
                                            scale=inv_late[:, t:t + 1])
                last.then_inc(done, 1)

            def copy_xT(g, near):
                if isinstance(g, int) and g >= UNITS:
                    return
                before = block_of(g - 1, near)
                for u in range(KT):
                    act_e.wait_ge(x_turned, 2 * g + u + 1)
                    if known(g) and u == 0:
                        act_e.wait_ge(scored, g)
                        if not by_rows(g - 1, before):
                            act_e.wait_ge(s_scored, s_unit(g - 1, before) + 1)
                        if before in PROJ:
                            act_e.wait_ge(projected, proj_unit(g - 1, before) + 1)
                    act_e.activation(xT[:, u, :], TR[u][:, :], ACT.Copy).then_inc(xT_ready, 1)

            def step(k, prev, cur, mid, front):
                g = k + 1
                if cur in FFN:
                    for ft in range(4):
                        gelu(k, cur, ft)
                if k_is(k, -2):
                    copy_xT(0, 0)
                if cur in FFN:
                    exps_steep(g, cur)
                    exps_flat(g, mid)
                if cur in PROJ:
                    act_e.wait_ge(mixed, 2 * (k + 1))
                    act_e.wait_ge(inv_kept, y_store(k, cur) + 1)
                    if known(k):
                        act_e.wait_ge(y_ready, k)
                    if k_is(k, 0):
                        act_e.wait_ge(chunk_split, 4)
                    if k_is(k, LAST):
                        act_e.wait_ge(y_saved, 16 * 2 * PAIRS)
                    elu_part(elu_r, ACT.Relu, elu_pos)
                    elu_part(elu_e, ACT.Exp, elu_exp)
                if cur in FFN:
                    for ft in range(4, FT - 1):
                        gelu(k, cur, ft)
                if mid is not None:
                    act_e.wait_ge(attn_turned, 2 * g + 1)
                    if known(g):
                        act_e.wait_ge(mixed, 2 * g)
                    act_e.activation(attnT[:, 0, :, :].rearrange("p a n -> p (a n)"), TR[0][:, :], ACT.Copy)\
                        .then_inc(attnT_a, 1)
                if cur in FFN:
                    gelu(k, cur, FT - 1)
                if cur in FFN:
                    copy_xT(k + 2, front)
                early = mid not in FFN and front is not None
                if early and cur not in FFN and front in (4, 5):
                    exps_steep(k + 2, mid)
                    exps_flat(k + 2, front)
                if mid not in FFN:
                    copy_xT(k + 3, front)
                if early and not (cur not in FFN and front in (4, 5)):
                    exps_steep(k + 2, mid)
                    if front != 0:
                        exps_flat(k + 2, front)
                if k_is(k, FFN0 - 1):
                    act_e.wait_ge(vec_ready, 1)
                if mid in FFN:
                    f = g - FFN0
                    for u in range(KT):
                        act_e.wait_ge(n_turned, 2 * f + u + 1)
                        cg, cb = V_G1 + (mid - 1) * KT + u, V_BETA1 + (mid - 1) * KT + u
                        act_e.activation(hT[:, u, :], TR[u][:, :], ACT.Identity, bias=vec[:, cb:cb + 1],
                                         scale=vec[:, cg:cg + 1]).then_inc(hT_ready, 1)
                if front in PROJ:
                    a = proj_unit(k + 2, front)
                    act_e.wait_ge(projected, a + 1)
                    if known(k + 2):
                        act_e.wait_ge(mixed, 2 * (k + 2))
                    if front == TOPK and isinstance(k, int):
                        act_e.wait_ge(outer_added, PAIRS)
                    for c in range(2):
                        act_e.activation(values[:, 2 * c:2 * c + 2, :].rearrange("p a n -> p (a n)"), ACC[c][:, :],
                                         ACT.Copy).then_inc(values_ready, 1)
                if front == 0:
                    exps_flat(k + 2, front)

            drive(act_e, step)

        @block.vector
        def _(dve):
            dve.memset(score_b[:, 0:1], 0.0)
            dve.memset(score_b[:, 5:6], 0.0)
            def project_vectors(i):
                dve.wait_ge(wproj_in, 16 * (3 if i == 0 else 5))
                for j in range(2):
                    for c in range(KT):
                        last = dve.tensor_tensor_reduce(out=(masked, y2)[i][:, 2 * j + c, :], in0=w_proj[:, c, :], in1=a_rows[:, j, :],
                                                        scale=1.0, scalar=0.0, op0=ALU.mult, op1=ALU.add,
                                                        accum_out=wa[:, i, j, c:c + 1])
                last.then_inc(wa_ready, 1)
                dve.wait_ge(wa_ready, 2 * i + 1)

            def prepare(b):
                if b == TOPK:
                    dve.wait_ge(y2_saved, 16 * LAYERS * PAIRS)
                    project_vectors(1)
                if b >= 2:
                    dve.wait_ge(scored, (b - 1) * PAIRS)
                dve.tensor_scalar(dst_rep[:, b % 2, :, :], columns(b, 1).unsqueeze(2).to_broadcast([P, KT, P]),
                                  1.0 / BIG, None, ALU.mult).then_inc(prep_ready, 1)

            project_vectors(0)
            dve.sem_inc(wa_ready, 1)
            prepare(0)

            def split_quarter(l, q, raw, count, n=0):
                dve.wait_ge(chunk_in[n], 16 * count)
                raw = raw[:, :, :].rearrange("p t n -> p (t n)")
                if q < 2:
                    hi, lo = w1_hi[:, q, :], w1_lo[:, q, :]
                else:
                    hi = w2_hi[:, 4 * (q - 2):4 * (q - 1), :].rearrange("p t n -> p (t n)")
                    lo = w2_lo[:, 4 * (q - 2):4 * (q - 1), :].rearrange("p t n -> p (t n)")
                dve.tensor_copy(hi, raw).then_inc(chunk_part, 1)
                dve.wait_ge(chunk_part, 4 * l + q + 1)
                dve.tensor_tensor(lo, raw, hi.bitcast(F32), ALU.subtract).then_inc(chunk_split, 1)

            def next_quarter(l, q):
                split_quarter(l, q, values, 2 + 4 * (l - 1) + q + 1)

            def layer_norm(i, n, buf):
                for t in range(T):
                    last = dve.bn_stats(stats[i][:, t, :], buf[:, t, :])
                last.then_inc(stats_done[i], 1)
                dve.wait_ge(stats_done[i], n + 1)
                dve.sem_inc(taken, 1)
                for t in range(T):
                    last = dve.bn_aggr(mean_var[i][:, t, :], stats[i][:, t, :])
                last.then_inc(moments[i], 1)
                dve.wait_ge(moments[i], n + 1)
                dve.tensor_scalar(var_eps[i][:, :], mean_var[i][:, :, 1], EPS, None, ALU.add).then_inc(var_ready[i], 1)

            def finish(i, n, buf, to=None):
                to = buf if to is None else to
                dve.wait_ge(rstd_ready[i], n + 1)
                for t in range(T):
                    last = dve.tensor_scalar(to[:, t, :], buf[:, t, :], mean_var[i][:, t, 0:1], rstd[i][:, t:t + 1],
                                             ALU.subtract, ALU.mult)
                last.then_inc(normed[i], 1)

            def scores(g, mid):
                if mid in PROJ:
                    a = proj_unit(g, mid)
                    dve.wait_ge(adj_loaded, 16 * (a + 1))
                    if known(g):
                        dve.wait_ge(max_ready, g)
                    if mid == 0 and known(g):
                        dve.wait_ge(loops_made, g)
                    dve.tensor_scalar(adj_mask[:, :, :], adj_in, 1.0, -1.0, ALU.is_lt, ALU.mult).then_inc(mask_made, 1)
                if by_rows(g, mid):
                    dve.wait_ge(s_summed, g + 1 - ROW_FIRST)
                else:
                    dve.wait_ge(s_scored, s_unit(g, mid) + 1)
                if known(g):
                    dve.wait_ge(bias_ready, g)
                dve.tensor_scalar(s_col[:, :], s_sum[:, :] if by_rows(g, mid) else S_BANK[:, 0:T], score_b[:, mid:mid + 1], None, ALU.add).then_inc(s_ready, 1)
                if mid in PROJ:
                    dve.wait_ge(mask_made, proj_unit(g, mid) + 1)
                else:
                    dve.wait_ge(mask_in, 16 * (g - PAIRS + 1))
                dve.wait_ge(scored, g + 1)
                if known(g):
                    dve.wait_ge(attn_ready, g)
                dve.sem_inc(taken, 1)
                for t in range(T):
                    last = dve.tensor_tensor_reduce(out=masked[:, t, :], in0=D_BANK[:, (t // KT) * N:(t // KT + 1) * N],
                                                    in1=adj_mask[:, t, :], scale=BIG, scalar=-3.0e38, op0=ALU.add,
                                                    op1=ALU.max, accum_out=row_max[:, t:t + 1])
                last.then_inc(max_ready, 1)
                dve.wait_ge(max_ready, g + 1)
                dve.wait_ge(s_ready, g + 1)
                dve.tensor_tensor(z_max[:, :], s_col[:, :], row_max[:, :], ALU.add).then_inc(z_ready, 1)
                dve.wait_ge(z_ready, g + 1)
                dve.scalar_tensor_tensor(out=m_col[:, :], in0=z_max[:, :], scalar=ALPHA[mid], in1=z_max[:, :],
                                         op0=ALU.mult, op1=ALU.max).then_inc(m_ready, 1)
                dve.wait_ge(m_ready, g + 1)
                if known(g):
                    dve.wait_ge(exps_done, g)
                dve.tensor_tensor(exp_bias[:, 0, :], s_col[:, :], m_col[:, :], ALU.subtract)
                dve.scalar_tensor_tensor(out=exp_bias[:, 1, :], in0=s_col[:, :], scalar=ALPHA[mid], in1=m_col[:, :],
                                         op0=ALU.mult, op1=ALU.subtract).then_inc(bias_ready, 1)

            def source_sums(g, front):
                dve.wait_ge(xs_in, 16 * (g + 1))
                dve.wait_ge(src_in, 16 * len(ROW_S))
                dve.wait_ge(s_ready, g)
                dve.wait_ge(attn_ready, g)
                dve.sem_inc(taken, 1)
                for t in range(T):
                    last = dve.tensor_tensor_reduce(out=masked[:, t, :], in0=x_front[:, t, :], in1=a_rows[:, front - 1, :],
                                                    scale=1.0, scalar=0.0, op0=ALU.mult, op1=ALU.add,
                                                    accum_out=s_sum[:, t:t + 1])
                last.then_inc(s_summed, 1)

            def weights(g, mid):
                dve.wait_ge(exps_done, g + 1)
                if known(g):
                    dve.wait_ge(inv_ready, g)
                for t in range(T):
                    last = dve.scalar_tensor_tensor(out=attn[:, t, :], in0=attn[:, t, :], scalar=1.0, in1=masked[:, t, :],
                                                    op0=ALU.mult, op1=ALU.max, accum_out=row_sum[:, t:t + 1])
                last.then_inc(weights_made, 1)
                dve.wait_ge(weights_made, g + 1)
                if mid == TOPK:
                    n = 3 * (g - LAST)
                    dve.sem_inc(taken, 1)
                    for t in range(T):
                        last = dve.max(top_a[:, t, :], attn[:, t, :])
                    last.then_inc(top_step, 1)
                    dve.wait_ge(top_step, n + 1)
                    dve.sem_inc(taken, 1)
                    for t in range(T):
                        last = dve.match_replace(masked[:, t, :], top_a[:, t, :], attn[:, t, :], -1.0)
                    last.then_inc(top_step, 1)
                    dve.wait_ge(top_step, n + 2)
                    dve.sem_inc(taken, 1)
                    for t in range(T):
                        last = dve.max(top_b[:, t, :], masked[:, t, :])
                    last.then_inc(top_step, 1)
                    dve.wait_ge(top_step, n + 3)
                dve.reciprocal(inv_sum[:, :], row_sum[:, :]).then_inc(inv_ready, 1)
                if mid == TOPK:
                    for t in range(T):
                        last = dve.scalar_tensor_tensor(out=attn[:, t, :], in0=attn[:, t, :], scalar=top_b[:, t, 7:8],
                                                        in1=attn[:, t, :], op0=ALU.is_ge, op1=ALU.mult)
                    last.then_inc(attn_ready, 1)
                else:
                    dve.sem_inc(attn_ready, 1)

            def copy_attnT(g):
                dve.wait_ge(attn_turned, 2 * g + 2)
                if known(g):
                    dve.wait_ge(mixed, 2 * g)
                dve.tensor_copy(attnT[:, 1, :, :].rearrange("p a n -> p (a n)"), TR[1][:, :]).then_inc(attnT_d, 1)

            def keep_inverse(g, b):
                dve.wait_ge(inv_ready, g + 1)
                if b in PROJ and known(g):
                    dve.wait_ge(elu_exp, proj_unit(g, b))
                dve.tensor_copy(inv_late[:, :], inv_sum[:, :]).then_inc(inv_kept, 1)

            def elu_first(g, b):
                a = proj_unit(g, b)
                dve.wait_ge(elu_pos, a + 1)
                dve.wait_ge(xm_in, 16 * (g + 1))
                dve.scalar_tensor_tensor(out=elu_r[:, :, :], in0=elu_r[:, :, :], scalar=-1.0, in1=x_mix[:, :, :],
                                         op0=ALU.add, op1=ALU.add).then_inc(elu_sum, 1)

            def residual(g, before, b):
                if before in FFN:
                    dve.wait_ge(res_scaled, g - FFN0)
                elif before == BLOCKS - 2:
                    dve.wait_ge(normed[0], g)
                elif before == BLOCKS - 1:
                    dve.wait_ge(out_saved, 16 * (g - LAST))
                elif before is not None:
                    if k_is(g, PAIRS):
                        dve.wait_ge(normed[0], g)
                    else:
                        dve.wait_ge(y_saved, 16 * g)
                        dve.wait_ge(outer_saved, 16 * g)
                if k_is(g, 0):
                    dve.wait_ge(bb_ready, 1)
                if b in PROJ:
                    a = proj_unit(g, b)
                    dve.wait_ge(elu_exp, a + 1)
                    dve.wait_ge(elu_sum, a + 1)
                    dve.scalar_tensor_tensor(out=y[:, :, :], in0=elu_e[:, :, :], scalar=1.0, in1=elu_r[:, :, :],
                                             op0=ALU.min, op1=ALU.add).then_inc(y_ready, 1)
                else:
                    if b in FFN:
                        dve.wait_ge(inv_ready, g + 1)
                    else:
                        dve.wait_ge(inv_kept, y_store(g, b) + 1)
                    inv = inv_sum if b in FFN else inv_late
                    dve.wait_ge(xm_in, 16 * (g + 1))
                    for t in range(T):
                        if t % 2 == 0:
                            dve.wait_ge(mixed, 2 * g + t // 2 + 1)
                        last = dve.scalar_tensor_tensor(out=y[:, t, :], in0=MIXB[t // 2][:, (t % 2) * D:(t % 2 + 1) * D],
                                                        scalar=inv[:, t:t + 1], in1=x_mix[:, t, :],
                                                        op0=ALU.mult, op1=ALU.add)
                    last.then_inc(y_ready, 1)

            def moments_of_y(g):
                dve.wait_ge(y_ready, g + 1)
                layer_norm(0, g, y)

            def split_h(g):
                f = g - FFN0
                for u in range(KT):
                    dve.wait_ge(hT_ready, 2 * f + u + 1)
                    if known(f) and u == 0:
                        dve.wait_ge(hid_done, FT * f)
                    dve.tensor_copy(h_hi[:, u, :], hT[:, u, :]).then_inc(h_hi_ready, 1)
                    dve.wait_ge(h_hi_ready, 2 * f + u + 1)
                    dve.tensor_tensor(h_lo[:, u, :], hT[:, u, :], h_hi[:, u, :].bitcast(F32), ALU.subtract)\
                        .then_inc(h_ready, 1)

            def split_act(k, ft):
                f = k - FFN0
                dve.wait_ge(act_ready, FT * f + ft + 1)
                if ft >= 4 or known(f):
                    dve.wait_ge(ff_done, FT * f + ft - 3)
                dve.tensor_copy(act_hi[:, ft % 4, :], act[:, ft % 2, :]).then_inc(act_hi_ready, 1)
                dve.wait_ge(act_hi_ready, FT * f + ft + 1)
                dve.tensor_tensor(act_lo[:, ft % 4, :], act[:, ft % 2, :], act_hi[:, ft % 4, :].bitcast(F32),
                                  ALU.subtract).then_inc(act_split, 1)

            def step(k, prev, cur, mid, front):
                if isinstance(k, int) and k % PAIRS == PAIRS - 2 and 0 < k and k // PAIRS + 1 in range(2, BLOCKS):
                    prepare(k // PAIRS + 1)
                if cur is not None and cur not in FFN:
                    keep_inverse(k, cur)
                if cur in FFN:
                    scores(k + 1, mid)
                new_layer = cur in FFN and cur != FFN[0] and k_is(k, cur * PAIRS)
                last_unit = cur in FFN and cur != FFN[-1] and k_is(k, cur * PAIRS + PAIRS - 1)
                f1 = k - 1 - FFN0
                if prev == FFN[-1] and cur in FFN:
                    split_act(k, 0)
                    split_act(k, 1)
                if prev in FFN:
                    dve.wait_ge(ff_done, FT * (f1 + 1))
                    dve.wait_ge(res_ready, f1 + 1)
                    if known(f1):
                        dve.wait_ge(y2_saved, 16 * f1)
                    for c in range(2):
                        last = dve.tensor_tensor(y2[:, 2 * c:2 * c + 2, :].rearrange("p a n -> p (a n)"), ACC[c][:, :],
                                                 h_res[:, 2 * c:2 * c + 2, :].rearrange("p a n -> p (a n)"), ALU.add)
                    last.then_inc(y2_ready, 1)
                if new_layer:
                    dve.wait_ge(ff_done, FT * (k - FFN0))
                    next_quarter(cur - 1, 2)
                if cur in FFN and prev != FFN[-1]:
                    split_act(k, 0)
                    split_act(k, 1)
                if prev in FFN:
                    dve.wait_ge(y2_ready, f1 + 1)
                    layer_norm(1, f1, y2)
                if cur in FFN:
                    split_act(k, 2)
                    split_act(k, 3)
                if prev in FFN:
                    finish(1, f1, y2)
                if mid is not None:
                    weights(k + 1, mid)
                if new_layer:
                    next_quarter(cur - 1, 3)
                if k_is(k, 0):
                    dve.wait_ge(vec_mm, 1)
                    dve.tensor_copy(vec[:, :], TR[0][:, 0:V_ROWS]).then_inc(vec_ready, 1)
                    dve.wait_ge(vec_ready, 1)
                    prepare(1)
                if cur in PROJ:
                    elu_first(k, cur)
                elif cur is not None and cur not in FFN:
                    residual(k, prev, cur)
                if cur == TOPK:
                    residual(k, prev, cur)
                if cur in FFN:
                    split_act(k, 4)
                if mid is not None:
                    copy_attnT(k + 1)
                if cur in FFN:
                    split_act(k, 5)
                    split_act(k, 6)
                if last_unit:
                    dve.wait_ge(hid_done, FT * (k - FFN0 + 1))
                    next_quarter(cur, 0)
                early = mid not in FFN and front is not None
                if early and cur not in FFN:
                    scores(k + 2, front)
                if cur == 0:
                    residual(k, prev, cur)
                if cur is not None and cur not in FFN:
                    moments_of_y(k)
                if k_is(k, PAIRS - 1):
                    dve.wait_ge(mixed, 2 * PAIRS)
                if cur in PROJ:
                    finish(0, k, y, values if k_is(k, PAIRS - 1) else y)
                elif cur is not None and cur not in FFN:
                    if known(k, 4 * PAIRS + 1):
                        dve.wait_ge(y_saved, 16 * y_store(k, cur))
                    finish(0, k, y, normed_avg)
                if mid in FFN:
                    residual(k + 1, cur, mid)
                    moments_of_y(k + 1)
                if cur in FFN:
                    split_act(k, 7)
                if mid in FFN:
                    finish(0, k + 1, y)
                if cur in FFN and by_rows(k + 2, front):
                    source_sums(k + 2, front)
                if prev == FFN[-1]:
                    n = k - 1 - prev * PAIRS
                    dve.wait_ge(outer_added, n + 1)
                    layer_norm(2, n, y2)
                if mid in FFN:
                    split_h(k + 1)
                if last_unit:
                    next_quarter(cur, 1)
                if k_is(k, -1):
                    for q in range(4):
                        split_quarter(0, q, (h_res, y2)[q % 2], q // 2 + 1, q % 2)
                if prev == FFN[-1]:
                    finish(2, n, y2)
                if early and cur in FFN:
                    scores(k + 2, front)

            drive(dve, step)

        @block.tensor
        def _(pe):
            pe.wait_ge(ident_ready, 2)

            def hidden(k, ft):
                f = k - FFN0
                if ft >= 4:
                    pe.wait_ge(act_ready, FT * f + ft - 3)
                if ft == 2:
                    pe.wait_ge(s_ready, k + 2)
                if ft == 3:
                    pe.wait_ge(max_ready, k + 2)
                o = HID[ft % 4][:, :]
                for c in range(KT):
                    if ft == 0:
                        pe.wait_ge(h_ready, 2 * f + c + 1)
                    if ft == 0 and isinstance(k, int) and k % PAIRS == 0:
                        pe.wait_ge(chunk_split, 4 * (k // PAIRS - 1) + c + 1)
                    col = slice(ft * P, (ft + 1) * P)
                    pe.matmul(o, w1_hi[:, c, col], h_hi[:, c, :], start=(c == 0), stop=False)
                    pe.matmul(o, w1_hi[:, c, col], h_lo[:, c, :], start=False, stop=False)
                    last = pe.matmul(o, w1_lo[:, c, col], h_hi[:, c, :], start=False, stop=(c == KT - 1))
                last.then_inc(hid_done, 1)

            def down(k, ft):
                f = k - FFN0
                pe.wait_ge(act_split, FT * f + ft + 1)
                if ft == 0 and known(f):
                    pe.wait_ge(y2_ready, f)
                for t in range(T):
                    o = ACC[t // 2][:, (t % 2) * D:(t % 2 + 1) * D]
                    col = slice(t * P, (t + 1) * P)
                    pe.matmul(o, act_hi[:, ft % 4, col], w2_hi[:, ft, :], start=(ft == 0 and t % 2 == 0), stop=False,
                              skip_group_check=True)
                    pe.matmul(o, act_hi[:, ft % 4, col], w2_lo[:, ft, :], start=False, stop=False, skip_group_check=True)
                    last = pe.matmul(o, act_lo[:, ft % 4, col], w2_hi[:, ft, :], start=False, stop=(ft == FT - 1),
                                     skip_group_check=True)
                last.then_inc(ff_done, 1)

            def turn_attn(g):
                pe.wait_ge(attn_ready, g + 1)
                for u in range(2):
                    for j in range(KT):
                        for i in range(KT):
                            last = pe.transpose(TR[u][:, (j * KT + i) * P:(j * KT + i + 1) * P],
                                                attn[:, u * KT + i, j * P:(j + 1) * P], ident[:, :])
                    last.then_inc(attn_turned, 1)

            def mix(k, g, cur, mid, u):
                if u == 0:
                    if mid in PROJ:
                        pe.wait_ge(values_ready, 2 * (proj_unit(g, mid) + 1))
                    elif own_values(g, mid):
                        pe.wait_ge(av_in, 16 * (g - AVG_FIRST + 1))
                    else:
                        pe.wait_ge(xm_in, 16 * (g + 1))
                    if cur in FFN:
                        pe.wait_ge(act_ready, FT * (k - FFN0) + 6)
                    elif cur in PROJ:
                        pe.wait_ge(elu_exp, proj_unit(k, cur) + 1)
                    elif cur is not None:
                        pe.wait_ge(y_ready, g)
                v = values if mid in PROJ or own_values(g, mid) else x_mix
                pe.wait_ge(attnT_a if u == 0 else attnT_d, g + 1)
                for i in range(KT):
                    for j in range(KT):
                        last = pe.matmul(MIXB[u][:, i * D:(i + 1) * D], attnT[:, u, j, i * P:(i + 1) * P],
                                         v[:, u * KT + j, :], start=(j == 0), stop=(j == KT - 1))
                last.then_inc(mixed, 1)

            def turn_x(g, after=None):
                if isinstance(g, int) and g >= UNITS:
                    return
                pe.wait_ge(xs_in, 16 * (g + 1))
                if after is not None:
                    pe.wait_ge(attnT_a, after + 1)
                    pe.wait_ge(attnT_d, after + 1)
                elif known(g):
                    pe.wait_ge(xT_ready, 2 * g)
                for u in range(KT):
                    for t in range(T):
                        last = pe.transpose(TR[u][:, t * P:(t + 1) * P], x_front[:, t, u * P:(u + 1) * P], ident[:, :])
                    last.then_inc(x_turned, 1)

            def target_scores(k, g, cur, front):
                pe.wait_ge(xT_ready, 2 * g + 2)
                if isinstance(g, int) and g % PAIRS == 0:
                    pe.wait_ge(prep_ready, g // PAIRS + 1)
                if cur in FFN:
                    pe.wait_ge(act_ready, FT * (k - FFN0) + FT)
                elif known(g):
                    pe.wait_ge(max_ready, g)
                for c in range(KT):
                    last = pe.matmul(D_BANK[:, :], dst_rep[:, front % 2, c, :], xT[:, c, :], start=(c == 0),
                                     stop=(c == KT - 1))
                last.then_inc(scored, 1)

            def source_scores(k, g, cur, front):
                if cur in FFN:
                    pe.wait_ge(act_ready, FT * (k - FFN0) + FT - 1)
                elif known(g):
                    pe.wait_ge(s_ready, g)
                for t in range(T):
                    for c in range(KT):
                        last = pe.matmul(S_BANK[:, t:t + 1], xT[:, c, t * P:(t + 1) * P], columns(front, 0)[:, c:c + 1],
                                         start=(c == 0), stop=(c == KT - 1))
                last.then_inc(s_scored, 1)

            def project(k, g, front):
                a = proj_unit(g, front)
                pe.wait_ge(xT_ready, 2 * g + 2)
                if known(a):
                    pe.wait_ge(values_ready, 2 * a)
                if front == 0 and isinstance(g, int) and g == 0:
                    pe.wait_ge(prep_ready, 1)
                if front == TOPK and isinstance(g, int):
                    pe.wait_ge(prep_ready, TOPK + 1)
                    pe.wait_ge(y2_ready, 3 * PAIRS)
                for t in range(T):
                    for c in range(KT):
                        last = pe.matmul(ACC[t // 2][:, (t % 2) * D:(t % 2 + 1) * D], xT[:, c, t * P:(t + 1) * P],
                                         w_proj[:, c, :], start=(c == 0), stop=(c == KT - 1))
                last.then_inc(projected, 1)

            def step(k, prev, cur, mid, front):
                g, g2 = k + 1, k + 2
                if cur in FFN:
                    for ft in range(4):
                        hidden(k, ft)
                    for ft in range(4):
                        if ft == 3:
                            turn_attn(g)
                        hidden(k, ft + 4)
                        if ft == 3:
                            mix(k, g, cur, mid, 0)
                            mix(k, g, cur, mid, 1)
                        if ft == 0 and k_is(k, cur * PAIRS):
                            pe.wait_ge(chunk_split, 4 * (cur - 1) + 3)
                        down(k, ft)
                    if k_is(k, cur * PAIRS):
                        pe.wait_ge(chunk_split, 4 * cur)
                    down(k, 4)
                    down(k, 5)
                    turn_x(g2, g)
                    down(k, 6)
                else:
                    if k_is(k, -2):
                        turn_x(0)
                    if front is not None:
                        target_scores(k, g2, cur, front)
                    if front in PROJ:
                        project(k, g2, front)
                    if front in (4, 5):
                        source_scores(k, g2, cur, front)
                    if k_is(k, 0):
                        pe.wait_ge(consts_in, 16 * CONSTS)
                        pe.transpose(TR[0][:, 0:V_ROWS], vec_rows[:, :], ident[0:V_ROWS, 0:V_ROWS]).then_inc(vec_mm, 1)
                        pe.wait_ge(vec_ready, 1)
                    if mid is not None:
                        turn_attn(g)
                    if front in (0, 1):
                        source_scores(k, g2, cur, front)
                    if mid is not None:
                        mix(k, g, cur, mid, 0)
                    if mid not in FFN:
                        turn_x(k + 3, None if mid is None else g)
                    if mid is not None:
                        mix(k, g, cur, mid, 1)
                if mid in FFN:
                    pe.wait_ge(normed[0], g + 1)
                    if cur in FFN:
                        pe.wait_ge(xT_ready, 2 * g2 + 2)
                    for u in range(KT):
                        for t in range(T):
                            last = pe.transpose(TR[u][:, t * P:(t + 1) * P], y[:, t, u * P:(u + 1) * P], ident[:, :])
                        last.then_inc(n_turned, 1)
                if cur in FFN:
                    down(k, 7)
                    target_scores(k, g2, cur, front)
                    if not by_rows(g2, front):
                        source_scores(k, g2, cur, front)
                    if mid not in FFN:
                        turn_x(k + 3)

            drive(pe, step)


_INS = ['x', 'adj', 'L0_gnn_w', 'L0_gnn_a1', 'L0_gnn_a2', 'L1_gnn_attn_w', 'L1_gnn_attn_b', 'L1_gnn_W1', 'L1_gnn_b1',
        'L1_gnn_W2', 'L1_gnn_b2', 'L1_gnn_g1', 'L1_gnn_beta1', 'L1_gnn_g2', 'L1_gnn_beta2', 'L2_gnn_attn_w_src',
        'L2_gnn_attn_w_dst', 'L2_gnn_attn_b', 'L3_gnn_W', 'L3_gnn_a']
_OUTS = [((GRAPHS, N, D), 'float32')]


def kernel(**inputs):
    import numpy as _np
    import concourse.bacc as _bacc
    from concourse import mybir as _mybir
    from concourse.bass_utils import run_bass_kernel_spmd as _run

    nc = _bacc.Bacc("TRN2", target_bir_lowering=False, num_devices=1)
    arrays, args = {}, []
    for name in _INS:
        a = _np.ascontiguousarray(inputs[name])
        arrays[f"in_{name}_dram"] = a
        args.append(nc.dram_tensor(f"in_{name}_dram", a.shape, _mybir.dt.from_np(a.dtype), kind="ExternalInput").ap())
    for i, (shape, dtype) in enumerate(_OUTS):
        dt = _mybir.dt.from_np(_np.dtype(dtype))
        args.append(nc.dram_tensor(f"out_{i}_dram", shape, dt, kind="ExternalOutput").ap())
    graph_stack(nc, *args)
    r = _run(nc, [arrays], core_ids=[0])
    got = tuple(r.results[0][f"out_{i}_dram"] for i in range(len(_OUTS)))
    return got[0]
```

```python
import concourse.bass as bass
from concourse import mybir
from contextlib import ExitStack

F32 = mybir.dt.float32
F32R = mybir.dt.float32r
I32 = mybir.dt.int32
I8 = mybir.dt.int8
ALU = mybir.AluOpType
ACT = mybir.ActivationFunctionType

P = 128
GRAPHS, N, D = 32, 256, 256
PAIRS = GRAPHS // 2
T = 2 * N // P
KT = D // P
TOK = 2 * N
LAYERS, FF = 3, 1024
FT = FF // P
BLOCKS = 6
UNITS = BLOCKS * PAIRS
FFN = (1, 2, 3)
PROJ = (0, 5)
TOPK = 5
ROW_FIRST = PAIRS + 2
ROW_LAST = 4 * PAIRS - 1
AVG_FIRST = 4 * PAIRS + 2
ALPHA = (0.1, 0.2, 0.2, 0.2, 0.2, 0.2)
EPS = 1e-5
BIG = 2.0 ** 64
FFN0 = FFN[0] * PAIRS
LAST = UNITS - PAIRS

CONSTS = 13
V_ATT, V_B1, V_G1, V_BETA1, V_SRC, V_DST, V_ROWS = 0, 12, 36, 42, 48, 50, 52


def graph_stack(nc, x, adj, w0, a0_src, a0_dst, attn_w, attn_b, w1, b1, w2, b2, g1, beta1, g2, beta2,
                l2_src, l2_dst, l2_b, w3, a3, out):
    x_t = x.rearrange("b (i p) d -> p (b i) d", p=P)
    adj_t = adj.rearrange("b (i p) j -> p (b i) j", p=P)
    out_t = out.rearrange("b (i p) d -> p (b i) d", p=P)
    x_outer = nc.dram_tensor("x_outer", (P, PAIRS * T, D), F32, kind="Internal").ap()

    ctx = ExitStack()
    with ctx:
        def sb(name, shape, dt=F32):
            return ctx.enter_context(nc.sbuf_tensor(name, shape, dt))

        def sem(name):
            return ctx.enter_context(nc.semaphore(name))

        state = sb("state", [P, PAIRS * T, D])
        edges = sb("edges", [P, PAIRS * T, N], I8)
        w1_hi = sb("w1_hi", [P, KT, FF], F32R)
        w1_lo = sb("w1_lo", [P, KT, FF], F32R)
        w2_hi = sb("w2_hi", [P, FT, D], F32R)
        w2_lo = sb("w2_lo", [P, FT, D], F32R)
        w_proj = sb("w_proj", [P, KT, D])
        a_rows = sb("a_rows", [P, 2, D])
        wa = sb("wa", [P, 2, 2, KT])
        dst_rep = sb("dst_rep", [P, 2, KT, P])
        vec_rows = sb("vec_rows", [V_ROWS, P])
        vec = sb("vec", [P, V_ROWS])
        score_b = sb("score_b", [P, BLOCKS])
        norm_w = sb("norm_w", [P, LAYERS, 4, D])
        ident = sb("ident", [P, P])
        neg_half = sb("neg_half", [P, T])
        unused = sb("unused", [P, 1])
        x_front = sb("x_front", [P, T, D])
        x_mix = sb("x_mix", [P, T, D])
        xT = sb("xT", [P, KT, TOK])
        adj_mask = sb("adj_mask", [P, T, N], I8)
        loop_mask = sb("loop_mask", [P, T, N], I8)
        masked = sb("masked", [P, T, N])
        attn = sb("attn", [P, T, N])
        attnT = sb("attnT", [P, 2, KT, N])
        y = sb("y", [P, T, D])
        values = sb("values", [P, T, D])
        h_hi = sb("h_hi", [P, KT, TOK], F32R)
        h_lo = sb("h_lo", [P, KT, TOK], F32R)
        h_res = sb("h_res", [P, T, D])
        act = sb("act", [P, 2, TOK])
        act_hi = sb("act_hi", [P, 4, TOK], F32R)
        act_lo = sb("act_lo", [P, 4, TOK], F32R)
        y2 = sb("y2", [P, T, D])
        s_sum = sb("s_sum", [P, T])
        d_sum = sb("d_sum", [P, T])
        s_col = sb("s_col", [P, T])
        row_max = sb("row_max", [P, T])
        z_max = sb("z_max", [P, T])
        m_col = sb("m_col", [P, T])
        exp_bias = sb("exp_bias", [P, 2, T])
        row_sum = sb("row_sum", [P, T])
        inv_sum = sb("inv_sum", [P, T])
        inv_late = sb("inv_late", [P, T])
        top_a = sb("top_a", [P, T, 8])
        top_b = sb("top_b", [P, T, 8])
        stats = [sb(f"stats{i}", [P, T, 6]) for i in range(3)]
        mean_var = [sb(f"mean_var{i}", [P, T, 2]) for i in range(3)]
        var_eps = [sb(f"var_eps{i}", [P, T]) for i in range(3)]
        rstd = [sb(f"rstd{i}", [P, T]) for i in range(3)]
        shift = sb("shift", [P, T])

        adj_in = act[:, :, :].bitcast(I32).rearrange("p a (t j) -> p (a t) j", j=N)
        hT = xT
        x_saved = values
        elu_e = y2
        elu_r = h_res
        normed_avg = h_res

        FIRST_RAW = PAIRS - 4
        first_raw = [state[:, (FIRST_RAW + q) * T:(FIRST_RAW + q + 1) * T, :] for q in range(4)]

        bank = [ctx.enter_context(nc.psum_tensor(f"bank{i}", [P, 512], F32)) for i in range(8)]
        TR = bank[0:2]
        ACC = bank[2:4]
        HID = bank[4:8]

        def banks(before, b):
            return (HID[2:4], HID[0], HID[1]) if before in FFN and b in FFN else (HID[0:2], HID[2], HID[3])

        consts_in = sem("consts_in")
        wproj_in = sem("wproj_in")
        chunk_in = [sem(f"chunk_in{i}") for i in range(4)]
        chunk_split = sem("chunk_split")
        chunk_part = sem("chunk_part")
        ident_ready = sem("ident_ready")
        vec_mm = sem("vec_mm")
        vec_ready = sem("vec_ready")
        wa_ready = sem("wa_ready")
        rows_in = sem("rows_in")
        prep_ready = sem("prep_ready")
        bb_ready = sem("bb_ready")
        xs_in = sem("xs_in")
        xm_in = sem("xm_in")
        av_in = sem("av_in")
        mask_in = sem("mask_in")
        adj_loaded = sem("adj_loaded")
        mask_made = sem("mask_made")
        loops_made = sem("loops_made")
        edges_saved = sem("edges_saved")
        y_saved = sem("y_saved")
        y2_saved = sem("y2_saved")
        outer_saved = sem("outer_saved")
        saved_in = sem("saved_in")
        out_saved = sem("out_saved")
        x_turned = sem("x_turned")
        xT_ready = sem("xT_ready")
        scored = sem("scored")
        s_scored = sem("s_scored")
        projected = sem("projected")
        values_ready = sem("values_ready")
        s_summed = sem("s_summed")
        d_summed = sem("d_summed")
        s_ready = sem("s_ready")
        max_ready = sem("max_ready")
        z_ready = sem("z_ready")
        m_ready = sem("m_ready")
        bias_ready = sem("bias_ready")
        table_in = sem("table_in")
        exps_done = sem("exps_done")
        weights_made = sem("weights_made")
        inv_ready = sem("inv_ready")
        top_step = sem("top_step")
        attn_ready = sem("attn_ready")
        attn_turned = sem("attn_turned")
        attnT_a = sem("attnT_a")
        attnT_d = sem("attnT_d")
        mixed = sem("mixed")
        inv_kept = sem("inv_kept")
        elu_pos = sem("elu_pos")
        elu_exp = sem("elu_exp")
        elu_sum = sem("elu_sum")
        y_ready = sem("y_ready")
        stats_done = [sem(f"stats_done{i}") for i in range(3)]
        moments = [sem(f"moments{i}") for i in range(3)]
        var_ready = [sem(f"var_ready{i}") for i in range(3)]
        rstd_ready = [sem(f"rstd_ready{i}") for i in range(3)]
        normed = [sem(f"normed{i}") for i in range(3)]
        shift_ready = sem("shift_ready")
        n_turned = sem("n_turned")
        hT_ready = sem("hT_ready")
        h_hi_ready = sem("h_hi_ready")
        h_ready = sem("h_ready")
        res_scaled = sem("res_scaled")
        res_ready = sem("res_ready")
        hid_done = sem("hid_done")
        act_ready = sem("act_ready")
        act_split = sem("act_split")
        ff_done = sem("ff_done")
        y2_ready = sem("y2_ready")
        x_scaled = sem("x_scaled")
        x_ready = sem("x_ready")
        outer_added = sem("outer_added")
        taken = sem("taken")

        block = ctx.enter_context(nc.Block())

        def rows(pair):
            return bass.ds(pair * T, T)

        def columns(b, which):
            if b in PROJ:
                return wa[:, PROJ.index(b), which, :]
            if b in FFN:
                c = V_ATT + ((b - 1) * 2 + which) * KT
                return vec[:, c:c + KT]
            c = V_DST if which else V_SRC
            return vec[:, c:c + KT]

        def proj_unit(g, b):
            return g if b == 0 else g - LAST + PAIRS

        def by_rows(g, b):
            return ROW_FIRST <= g <= ROW_LAST if isinstance(g, int) else b in FFN

        def s_unit(g, b):
            low = g < ROW_FIRST if isinstance(g, int) else b == 0
            return g if low else g - (ROW_LAST - ROW_FIRST + 1)

        def own_values(g, b):
            return b == 4 and (not isinstance(g, int) or g >= AVG_FIRST)

        def block_of(g, near):
            return near if not isinstance(g, int) else int(g // PAIRS) if 0 <= g < UNITS else None

        def y_store(g, b):
            return g - {0: 0, 4: 3 * PAIRS, 5: 3 * PAIRS}[b]

        def drive(eng, step):
            def of(g):
                return int(g // PAIRS) if 0 <= g < UNITS else None

            def straight(k):
                step(k, of(k - 1), of(k), of(k + 1), of(k + 2))

            for k in (-2, -1):
                straight(k)
            for b in range(BLOCKS):
                first = 3 if b == 0 else 2
                for p in range(first):
                    straight(b * PAIRS + p)
                with eng.Fori(first, PAIRS - 4) as p:
                    step(p + b * PAIRS, b, b, b, b)
                for p in range(PAIRS - 4, PAIRS):
                    straight(b * PAIRS + p)

        def k_is(k, n):
            return isinstance(k, int) and k == n

        def known(g, least=1):
            return not isinstance(g, int) or g >= least

        @block.sync
        def _(sp):
            ld = nc.allow_non_contiguous_dma(reason="small constants")
            ld.__enter__()
            sp.dma_start(x_front[:, :, :], x_t[:, 0:T, :]).then_inc(xs_in, 16)
            sp.dma_start(w_proj[:, :, :], w0.rearrange("(t p) n -> p t n", p=P)).then_inc(wproj_in, 16)
            for i, src in enumerate((a0_src, a0_dst)):
                sp.dma_start(a_rows[:, i, :], src.rearrange("n o -> o n").to_broadcast([P, D])).then_inc(wproj_in, 16)

            def load_constants():
                for base, src in ((V_ATT, attn_w.rearrange("l (r q) -> (l r) q", q=P)),
                                  (V_B1, b1.rearrange("l (r q) -> (l r) q", q=P)),
                                  (V_G1, g1.rearrange("l (r q) -> (l r) q", q=P)),
                                  (V_BETA1, beta1.rearrange("l (r q) -> (l r) q", q=P)),
                                  (V_SRC, l2_src.rearrange("(r q) -> r q", q=P)),
                                  (V_DST, l2_dst.rearrange("(r q) -> r q", q=P))):
                    sp.dma_start(vec_rows[base:base + src.shape[0], :], src).then_inc(consts_in, 16)
                sp.dma_start(score_b[:, 1:4], attn_b.unsqueeze(0).to_broadcast([P, LAYERS])).then_inc(consts_in, 16)
                sp.dma_start(score_b[:, 4:5], l2_b.unsqueeze(0).to_broadcast([P, 1])).then_inc(consts_in, 16)
                for i, src in enumerate((g1, beta1, g2, beta2)):
                    sp.dma_start(norm_w[:, :, i, :], src.unsqueeze(0).to_broadcast([P, LAYERS, D])).then_inc(consts_in, 16)
                sp.dma_start(y[:, 0:LAYERS, :], b2.unsqueeze(0).to_broadcast([P, LAYERS, D])).then_inc(consts_in, 16)
                sp.wait_ge(wa_ready, 1)
                load_rows(0)

            def load_rows(l):
                for i in range(2):
                    sp.dma_start(a_rows[:, i, :], attn_w[l:l + 1, i * D:(i + 1) * D].to_broadcast([P, D])).then_inc(rows_in, 16)

            def load_quarter(l, q, raw, n):
                if q < 2:
                    sp.dma_start(raw[:, :, :].rearrange("p t n -> p (t n)"), w1[l, q * P:(q + 1) * P, :])\
                        .then_inc(chunk_in[n], 16)
                else:
                    src = w2[l, (q - 2) * 4 * P:(q - 1) * 4 * P, :].rearrange("(t p) n -> p t n", p=P)
                    sp.dma_start(raw[:, :, :], src).then_inc(chunk_in[n], 16)

            def load_mask(g, b):
                if known(g):
                    sp.wait_ge(max_ready, g)
                if b == 1 and isinstance(g, int):
                    sp.wait_ge(loops_made, min(g, PAIRS))
                sp.wait_ge(edges_saved, 16 * (g - b * PAIRS + 1))
                sp.sem_inc(taken, 1)
                sp.dma_start(adj_mask[:, :, :], edges[:, rows(g - b * PAIRS), :]).then_inc(mask_in, 16)

            def load_adj(g, b):
                a = proj_unit(g, b)
                if known(a):
                    sp.wait_ge(mask_made, a)
                if b == TOPK and isinstance(g, int):
                    sp.wait_ge(act_split, FT * 3 * PAIRS)
                sp.sem_inc(taken, 1)
                sp.dma_start(adj_in, adj_t[:, rows(g - b * PAIRS), :]).then_inc(adj_loaded, 16)

            def load_x(g, b, dst, done):
                if b - 1 in FFN:
                    sp.wait_ge(y2_saved, (g - PAIRS - FFN0 + 1) * 16)
                elif b > 0:
                    sp.wait_ge(y_saved, (y_store(g - PAIRS, b - 1) + 1) * 16)
                sp.sem_inc(taken, 1)
                src = x_t if b == 0 else state
                sp.dma_start(dst[:, :, :], src[:, rows(g - b * PAIRS), :]).then_inc(done, 16)

            def load_front(g, near):
                if isinstance(g, int) and g >= UNITS:
                    return
                if by_rows(g - 1, near):
                    sp.wait_ge(d_summed, g - ROW_FIRST)
                else:
                    sp.wait_ge(x_turned, 2 * (s_unit(g - 1, near) + 1))
                sp.sem_inc(taken, 1)
                load_x(g, block_of(g, near), x_front, xs_in)

            def save_layer(g, b):
                if b == FFN[-1]:
                    sp.wait_ge(normed[2], g - b * PAIRS + 1)
                else:
                    sp.wait_ge(x_ready, g - FFN0 + 1)
                sp.sem_inc(taken, 1)
                sp.dma_start(state[:, rows(g - b * PAIRS), :], (x_saved if b == FFN[-1] else y2)[:, :, :])\
                    .then_inc(y2_saved, 16)

            def load_edges(g, near):
                b = block_of(g, near)
                if b in PROJ:
                    load_adj(g, b)
                elif b is not None:
                    load_mask(g, b)

            def step(k, prev, cur, mid, front):
                if k_is(k, -2):
                    load_edges(0, 0)
                    load_front(1, 0)
                if cur in FFN and k_is(k, cur * PAIRS) and cur != FFN[0]:
                    sp.wait_ge(chunk_split, 4 * (cur - 1) + 3)
                    load_quarter(cur - 1, 3, values, 0)
                if own_values(k + 1, mid):
                    sp.wait_ge(mixed, 2 * (k + 1))
                    sp.sem_inc(taken, 1)
                    if k_is(k, AVG_FIRST - 1):
                        sp.wait_ge(y2_saved, 16 * LAYERS * PAIRS)
                        sp.sem_inc(taken, 1)
                    sp.dma_start(values[:, :, :], state[:, rows(k + 1 - mid * PAIRS), :]).then_inc(av_in, 16)
                if mid in FFN and front is not None:
                    load_edges(k + 2, front)
                if prev in (1, 2) and cur in FFN:
                    save_layer(k - 1, prev)

                next_layer = cur in FFN and mid in FFN and k_is(k, cur * PAIRS + PAIRS - 1)
                if next_layer:
                    sp.wait_ge(chunk_split, 4 * cur + 1)
                    load_quarter(cur, 1, values, 0)
                if k_is(k, 4 * PAIRS):
                    sp.wait_ge(projected, PAIRS)
                    sp.wait_ge(d_summed, ROW_LAST - ROW_FIRST + 1)
                    sp.dma_start(w_proj[:, :, :], w3.rearrange("(t p) n -> p t n", p=P)).then_inc(wproj_in, 16)
                    sp.dma_start(a_rows[:, :, :], a3.rearrange("(h n) o -> o h n", h=2).to_broadcast([P, 2, D]))\
                      .then_inc(wproj_in, 16)
                if cur not in FFN and mid is not None:
                    if cur in PROJ:
                        sp.wait_ge(elu_sum, proj_unit(k, cur) + 1)
                    elif cur is not None:
                        sp.wait_ge(y_ready, k + 1)
                    sp.sem_inc(taken, 1)
                    load_x(k + 1, mid, x_mix, xm_in)
                if front == 0:
                    sp.wait_ge(loops_made, k + 3)
                    sp.sem_inc(taken, 1)
                    sp.dma_start(edges[:, rows(k + 2), :], loop_mask[:, :, :]).then_inc(edges_saved, 16)
                if cur not in FFN and front not in FFN and front is not None:
                    load_edges(k + 3, front)
                if cur not in FFN and mid not in FFN:
                    load_front(k + 4, front)
                if cur is not None and cur not in FFN:
                    sp.wait_ge(normed[0], k + 1)
                    sp.sem_inc(taken, 1)
                    if k_is(k, FIRST_RAW):
                        sp.wait_ge(chunk_split, 4)
                        sp.sem_inc(taken, 1)
                    where = rows(k - cur * PAIRS)
                    src = normed_avg if cur == 4 else values if k_is(k, PAIRS - 1) else y
                    if cur == BLOCKS - 1:
                        sp.dma_start(out_t[:, where, :], src[:, :, :]).then_inc(out_saved, 16)
                    else:
                        sp.dma_start(state[:, where, :], src[:, :, :]).then_inc(y_saved, 16)
                    if cur == 0:
                        sp.dma_start(x_outer[:, where, :], src[:, :, :]).then_inc(outer_saved, 16)
                if prev in FFN and cur not in FFN:
                    save_layer(k - 1, prev)
                if mid in FFN and front is not None:
                    sp.wait_ge(y_ready, k + 2)
                    load_x(k + 2, front, x_mix, xm_in)
                if cur in FFN:
                    load_front(k + 3, front)
                    if mid not in FFN:
                        load_front(k + 4, front)
                    if front not in FFN:
                        load_edges(k + 3, front)
                if prev == FFN[-1] and cur == FFN[-1]:
                    save_layer(k - 1, prev)
                if cur == FFN[-1]:
                    if known(k, FFN[-1] * PAIRS + 1):
                        sp.wait_ge(y2_saved, 16 * (k - FFN0))
                    else:
                        sp.wait_ge(outer_saved, 16 * PAIRS)
                    if k_is(k, FFN[-1] * PAIRS):
                        sp.wait_ge(chunk_split, 4 * LAYERS)
                    sp.sem_inc(taken, 1)
                    sp.dma_start(x_saved[:, :, :], x_outer[:, rows(k - cur * PAIRS), :]).then_inc(saved_in, 16)
                if k_is(k, -2):
                    load_constants()
                    for q in range(4):
                        load_quarter(0, q, first_raw[q], q)
                if cur in FFN and cur != FFN[-1] and k_is(k, cur * PAIRS + PAIRS - 2):
                    sp.wait_ge(chunk_split, 4 * cur)
                    load_quarter(cur, 0, values, 0)
                if cur in FFN and cur != FFN[-1] and k_is(k, cur * PAIRS + PAIRS - 3):
                    sp.wait_ge(d_summed, k + 3 - ROW_FIRST)
                    load_rows(cur)
                if next_layer:
                    sp.wait_ge(chunk_split, 4 * cur + 2)
                    load_quarter(cur, 2, values, 0)

            drive(sp, step)
            ld.__exit__(None, None, None)
            sp.wait_ge(out_saved, 16 * PAIRS)
            sp.wait_ge(outer_saved, 16 * PAIRS)

        @block.gpsimd
        def _(pool):
            pool.memset(neg_half[:, :], -0.5)
            pool.memset(ident[:, :], 0.0).then_inc(ident_ready, 1)
            pool.wait_ge(ident_ready, 1)
            pool.affine_select(out=ident[:, :], in_=ident[:, :], compare_op=ALU.not_equal, fill=1.0, base=0,
                               pattern=[[-1, P]], channel_multiplier=1).then_inc(ident_ready, 1)
            pool.wait_ge(ident_ready, 2)

            def rsqrt(i, n):
                pool.wait_ge(var_ready[i], n + 1)
                pool.tensor_tensor(rstd[i][:, :], var_eps[i][:, :], neg_half[:, :], ALU.pow).then_inc(rstd_ready[i], 1)

            def wide(l, i):
                return norm_w[:, l:l + 1, i, :].to_broadcast([P, T, D])

            def step(k, prev, cur, mid, front):
                if front == 0:
                    g = k + 2
                    pool.wait_ge(mask_made, g + 1)
                    if known(g):
                        pool.wait_ge(edges_saved, 16 * g)
                    pool.sem_inc(taken, 1)
                    pool.affine_select(out=loop_mask[:, :, :].rearrange("p (b i) j -> p b i j", b=2),
                                       in_=adj_mask[:, :, :].rearrange("p (b i) j -> p b i j", b=2),
                                       compare_op=ALU.not_equal, fill=0.0, base=0,
                                       pattern=[[0, 2], [P, KT], [-1, N]], channel_multiplier=1)\
                        .then_inc(loops_made, 1)
                if k_is(k, -1):
                    pool.wait_ge(consts_in, 16 * CONSTS)
                    pool.tensor_tensor(norm_w[:, :, 1, :], norm_w[:, :, 1, :], y[:, 0:LAYERS, :], ALU.add)\
                        .then_inc(bb_ready, 1)
                if prev in FFN:
                    rsqrt(1, k - 1 - FFN0)
                if cur in FFN:
                    f = k - FFN0
                    pool.wait_ge(normed[0], k + 1)
                    if known(f):
                        pool.wait_ge(y2_ready, f)
                    pool.tensor_tensor(h_res[:, :, :], y[:, :, :], wide(cur - 1, 0), ALU.mult).then_inc(res_scaled, 1)
                if prev in FFN:
                    f = k - 1 - FFN0
                    pool.wait_ge(normed[1], f + 1)
                    pool.tensor_tensor(y2[:, :, :], y2[:, :, :], wide(prev - 1, 2), ALU.mult).then_inc(x_scaled, 1)
                    pool.wait_ge(x_scaled, f + 1)
                    pool.tensor_tensor(y2[:, :, :], y2[:, :, :], wide(prev - 1, 3), ALU.add).then_inc(x_ready, 1)
                    if prev == FFN[-1]:
                        n = k - 1 - prev * PAIRS
                        pool.wait_ge(x_ready, f + 1)
                        pool.wait_ge(saved_in, 16 * (n + 1))
                        pool.tensor_tensor(y2[:, :, :], y2[:, :, :], x_saved[:, :, :], ALU.add).then_inc(outer_added, 1)
                if cur is not None and cur not in FFN:
                    rsqrt(0, k)
                if mid in FFN:
                    rsqrt(0, k + 1)
                if prev == FFN[-1]:
                    rsqrt(2, k - 1 - prev * PAIRS)
                if cur in FFN:
                    f = k - FFN0
                    pool.wait_ge(res_scaled, f + 1)
                    pool.tensor_tensor(h_res[:, :, :], h_res[:, :, :], wide(cur - 1, 1), ALU.add).then_inc(res_ready, 1)

            drive(pool, step)

        @block.scalar
        def _(act_e):

            def gelu(k, cur, ft):
                f = k - FFN0
                act_e.wait_ge(hid_done, FT * f + ft + 1)
                if ft >= 2 or known(f):
                    act_e.wait_ge(act_split, FT * f + ft - 1)
                c = V_B1 + (cur - 1) * FT + ft
                if ft >= 4 or known(f):
                    act_e.wait_ge(ff_done, FT * f + ft - 3)
                act_e.activation(act[:, ft % 2, :], HID[ft % 4][:, :], ACT.Gelu, bias=vec[:, c:c + 1])
                act_e.activation(act_hi[:, ft % 4, :], HID[ft % 4][:, :], ACT.Gelu, bias=vec[:, c:c + 1])\
                    .then_inc(act_ready, 1)

            def exps_steep(g):
                act_e.wait_ge(bias_ready, g + 1)
                if known(g):
                    act_e.wait_ge(attn_turned, 2 * g)
                for t in range(T):
                    act_e.activation(attn[:, t, :], masked[:, t, :], ACT.Exp, bias=exp_bias[:, 0, t:t + 1])

            def exps_flat(g, mid):
                for t in range(T):
                    last = act_e.activation(masked[:, t, :], masked[:, t, :], ACT.Exp,
                                            bias=exp_bias[:, 1, t:t + 1], scale=ALPHA[mid])
                last.then_inc(exps_done, 1)

            def elu_part(dst, func, done):
                for t in range(T):
                    last = act_e.activation(dst[:, t, :], HID[t // 2][:, (t % 2) * D:(t % 2 + 1) * D], func,
                                            scale=inv_late[:, t:t + 1])
                last.then_inc(done, 1)

            def copy_xT(g, near):
                if isinstance(g, int) and g >= UNITS or by_rows(g, near):
                    return
                before = block_of(g - 1, near)
                for u in range(KT):
                    act_e.wait_ge(x_turned, 2 * s_unit(g, near) + u + 1)
                    if known(g) and u == 0:
                        act_e.wait_ge(scored, g)
                        if not by_rows(g - 1, before):
                            act_e.wait_ge(s_scored, s_unit(g - 1, before) + 1)
                        if before in PROJ:
                            act_e.wait_ge(projected, proj_unit(g - 1, before) + 1)
                        if isinstance(g, int) and 4 * PAIRS <= g <= 4 * PAIRS + 1:
                            act_e.wait_ge(h_ready, 2 * (g - 2 - FFN0 + 1))
                    act_e.activation(xT[:, u, :], TR[u][:, :], ACT.Copy).then_inc(xT_ready, 1)

            def step(k, prev, cur, mid, front):
                g = k + 1
                inner = cur in FFN and mid in FFN
                if cur in FFN:
                    for ft in range(4):
                        gelu(k, cur, ft)
                if k_is(k, -2):
                    copy_xT(0, 0)
                if cur in PROJ:
                    act_e.wait_ge(mixed, 2 * (k + 1))
                    act_e.wait_ge(inv_kept, y_store(k, cur) + 1)
                    if known(k):
                        act_e.wait_ge(y_ready, k)
                    if k_is(k, LAST):
                        act_e.wait_ge(y_saved, 16 * 2 * PAIRS)
                    elu_part(elu_r, ACT.Relu, elu_pos)
                    elu_part(elu_e, ACT.Exp, elu_exp)
                if cur in FFN and not inner:
                    for ft in range(4, FT - 1):
                        gelu(k, cur, ft)
                if mid is not None:
                    act_e.wait_ge(attn_turned, 2 * g + 1)
                    if known(g):
                        act_e.wait_ge(mixed, 2 * g)
                    act_e.activation(attnT[:, 0, :, :].rearrange("p a n -> p (a n)"), TR[0][:, :], ACT.Copy)\
                        .then_inc(attnT_a, 1)
                    if inner:
                        act_e.wait_ge(attn_turned, 2 * g + 2)
                        act_e.activation(attnT[:, 1, :, :].rearrange("p a n -> p (a n)"), TR[1][:, :], ACT.Copy)\
                            .then_inc(attnT_d, 1)
                if inner and prev in FFN:
                    f1 = k - 1 - FFN0
                    act_e.wait_ge(shift_ready, f1 + 1)
                    act_e.wait_ge(rstd_ready[1], f1 + 1)
                    for t in range(T):
                        last = act_e.activation(y2[:, t, :], y2[:, t, :], ACT.Identity, bias=shift[:, t:t + 1],
                                                scale=rstd[1][:, t:t + 1])
                    last.then_inc(normed[1], 1)
                if inner:
                    gelu(k, cur, 4)
                    gelu(k, cur, 5)
                    copy_xT(k + 2, front)
                    gelu(k, cur, 6)
                    gelu(k, cur, 7)
                    if known(k, FFN0 + 1):
                        act_e.wait_ge(table_in, k - FFN0)
                    act_e.activation(unused[:, :], neg_half[:, 0:1], ACT.Exp).then_inc(table_in, 1)
                elif cur in FFN:
                    gelu(k, cur, 7)
                    copy_xT(k + 2, front)
                early = mid not in FFN and front is not None
                if early and cur not in FFN and front in (4, 5):
                    exps_steep(k + 2)
                    exps_flat(k + 2, front)
                if mid not in FFN:
                    copy_xT(k + 3, front)
                if early and not (cur not in FFN and front in (4, 5)):
                    exps_steep(k + 2)
                    if front != 0:
                        exps_flat(k + 2, front)
                if k_is(k, FFN0 - 1):
                    act_e.wait_ge(vec_ready, 1)
                    act_e.wait_ge(ident_ready, 2)
                if mid in FFN:
                    f = g - FFN0
                    for u in range(KT):
                        act_e.wait_ge(n_turned, 2 * f + u + 1)
                        if u == 0:
                            if known(f):
                                act_e.wait_ge(h_ready, 2 * f)
                            if not by_rows(k + 2, front):
                                act_e.wait_ge(scored, k + 3)
                                act_e.wait_ge(s_scored, s_unit(k + 2, front) + 1)
                        cg, cb = V_G1 + (mid - 1) * KT + u, V_BETA1 + (mid - 1) * KT + u
                        act_e.activation(hT[:, u, :], TR[u][:, :], ACT.Identity, bias=vec[:, cb:cb + 1],
                                         scale=vec[:, cg:cg + 1]).then_inc(hT_ready, 1)
                if mid in FFN:
                    exps_steep(k + 2)
                    exps_flat(k + 2, front)
                if front in PROJ:
                    a = proj_unit(k + 2, front)
                    act_e.wait_ge(projected, a + 1)
                    if known(k + 2):
                        act_e.wait_ge(mixed, 2 * (k + 2))
                    if front == TOPK and isinstance(k, int):
                        act_e.wait_ge(outer_added, PAIRS)
                    for c in range(2):
                        act_e.activation(values[:, 2 * c:2 * c + 2, :].rearrange("p a n -> p (a n)"), ACC[c][:, :],
                                         ACT.Copy).then_inc(values_ready, 1)
                if front == 0:
                    exps_flat(k + 2, front)

            drive(act_e, step)

        @block.vector
        def _(dve):
            dve.memset(score_b[:, 0:1], 0.0)
            dve.memset(score_b[:, 5:6], 0.0)

            def project_vectors(i):
                dve.wait_ge(wproj_in, 16 * (3 if i == 0 else 5))
                for j in range(2):
                    for c in range(KT):
                        last = dve.tensor_tensor_reduce(out=(masked, y2)[i][:, 2 * j + c, :], in0=w_proj[:, c, :],
                                                        in1=a_rows[:, j, :], scale=1.0, scalar=0.0,
                                                        op0=ALU.mult, op1=ALU.add, accum_out=wa[:, i, j, c:c + 1])
                last.then_inc(wa_ready, 1)
                dve.wait_ge(wa_ready, i + 1)

            def prepare(b):
                if b == TOPK:
                    dve.wait_ge(y2_saved, 16 * LAYERS * PAIRS)
                    project_vectors(1)
                if b >= 2:
                    dve.wait_ge(scored, (b - 1) * PAIRS)
                dve.tensor_scalar(dst_rep[:, b % 2, :, :], columns(b, 1).unsqueeze(2).to_broadcast([P, KT, P]),
                                  1.0 / BIG, None, ALU.mult).then_inc(prep_ready, 1)

            project_vectors(0)
            prepare(0)

            def split_quarter(l, q, raw, count, n=0):
                dve.wait_ge(chunk_in[n], 16 * count)
                raw = raw[:, :, :].rearrange("p t n -> p (t n)")
                if q < 2:
                    hi, lo = w1_hi[:, q, :], w1_lo[:, q, :]
                else:
                    hi = w2_hi[:, 4 * (q - 2):4 * (q - 1), :].rearrange("p t n -> p (t n)")
                    lo = w2_lo[:, 4 * (q - 2):4 * (q - 1), :].rearrange("p t n -> p (t n)")
                dve.tensor_copy(hi, raw).then_inc(chunk_part, 1)
                dve.wait_ge(chunk_part, 4 * l + q + 1)
                dve.tensor_tensor(lo, raw, hi.bitcast(F32), ALU.subtract).then_inc(chunk_split, 1)

            def next_quarter(l, q):
                split_quarter(l, q, values, 1 + 4 * (l - 1) + q + 1)

            def layer_norm(i, n, buf):
                for t in range(T):
                    last = dve.bn_stats(stats[i][:, t, :], buf[:, t, :])
                last.then_inc(stats_done[i], 1)
                dve.wait_ge(stats_done[i], n + 1)
                dve.sem_inc(taken, 1)
                for t in range(T):
                    last = dve.bn_aggr(mean_var[i][:, t, :], stats[i][:, t, :])
                last.then_inc(moments[i], 1)
                dve.wait_ge(moments[i], n + 1)
                dve.tensor_scalar(var_eps[i][:, :], mean_var[i][:, :, 1], EPS, None, ALU.add).then_inc(var_ready[i], 1)

            def finish(i, n, buf, to=None):
                to = buf if to is None else to
                dve.wait_ge(rstd_ready[i], n + 1)
                for t in range(T):
                    last = dve.tensor_scalar(to[:, t, :], buf[:, t, :], mean_var[i][:, t, 0:1], rstd[i][:, t:t + 1],
                                             ALU.subtract, ALU.mult)
                last.then_inc(normed[i], 1)

            def scores(g, mid, s_bank, d_bank):
                if mid in PROJ:
                    a = proj_unit(g, mid)
                    dve.wait_ge(adj_loaded, 16 * (a + 1))
                    if known(g):
                        dve.wait_ge(max_ready, g)
                    if mid == 0 and known(g):
                        dve.wait_ge(loops_made, g)
                    dve.tensor_scalar(adj_mask[:, :, :], adj_in, 1.0, -1.0, ALU.is_lt, ALU.mult).then_inc(mask_made, 1)
                if by_rows(g, mid):
                    dve.wait_ge(s_summed, g + 1 - ROW_FIRST)
                else:
                    dve.wait_ge(s_scored, s_unit(g, mid) + 1)
                if known(g):
                    dve.wait_ge(bias_ready, g)
                dve.tensor_scalar(s_col[:, :], s_sum[:, :] if by_rows(g, mid) else s_bank[:, 0:T],
                                  score_b[:, mid:mid + 1], None, ALU.add).then_inc(s_ready, 1)
                if mid in PROJ:
                    dve.wait_ge(mask_made, proj_unit(g, mid) + 1)
                else:
                    dve.wait_ge(mask_in, 16 * (g - PAIRS + 1))
                dve.wait_ge(scored, g + 1)
                if known(g):
                    dve.wait_ge(attn_ready, g)
                dve.sem_inc(taken, 1)
                for t in range(T):
                    last = dve.tensor_tensor_reduce(out=masked[:, t, :], in0=d_bank[:, (t // KT) * N:(t // KT + 1) * N],
                                                    in1=adj_mask[:, t, :], scale=BIG, scalar=-3.0e38, op0=ALU.add,
                                                    op1=ALU.max, accum_out=row_max[:, t:t + 1])
                last.then_inc(max_ready, 1)
                dve.wait_ge(max_ready, g + 1)
                dve.wait_ge(s_ready, g + 1)
                dve.tensor_tensor(z_max[:, :], s_col[:, :], row_max[:, :], ALU.add).then_inc(z_ready, 1)
                dve.wait_ge(z_ready, g + 1)
                dve.scalar_tensor_tensor(out=m_col[:, :], in0=z_max[:, :], scalar=ALPHA[mid], in1=z_max[:, :],
                                         op0=ALU.mult, op1=ALU.max).then_inc(m_ready, 1)
                dve.wait_ge(m_ready, g + 1)
                if known(g):
                    dve.wait_ge(exps_done, g)
                dve.tensor_tensor(exp_bias[:, 0, :], s_col[:, :], m_col[:, :], ALU.subtract)
                dve.scalar_tensor_tensor(out=exp_bias[:, 1, :], in0=s_col[:, :], scalar=ALPHA[mid], in1=m_col[:, :],
                                         op0=ALU.mult, op1=ALU.subtract).then_inc(bias_ready, 1)

            def row_sums(g, front):
                dve.wait_ge(xs_in, 16 * (g + 1))
                dve.wait_ge(rows_in, 16 * 2 * front)
                dve.wait_ge(s_ready, g)
                dve.wait_ge(attn_ready, g)
                dve.wait_ge(scored, g)
                for i, (sums, scale, done) in enumerate(((s_sum, 1.0, s_summed), (d_sum, 1.0 / BIG, d_summed))):
                    if i:
                        dve.wait_ge(s_summed, g + 1 - ROW_FIRST)
                    dve.sem_inc(taken, 1)
                    for t in range(T):
                        last = dve.tensor_tensor_reduce(out=masked[:, t, :], in0=x_front[:, t, :], in1=a_rows[:, i, :],
                                                        scale=scale, scalar=0.0, op0=ALU.mult, op1=ALU.add,
                                                        accum_out=sums[:, t:t + 1])
                    last.then_inc(done, 1)

            def weights(g, mid):
                dve.wait_ge(exps_done, g + 1)
                if known(g):
                    dve.wait_ge(inv_ready, g)
                for t in range(T):
                    last = dve.scalar_tensor_tensor(out=attn[:, t, :], in0=attn[:, t, :], scalar=1.0, in1=masked[:, t, :],
                                                    op0=ALU.mult, op1=ALU.max, accum_out=row_sum[:, t:t + 1])
                last.then_inc(weights_made, 1)
                dve.wait_ge(weights_made, g + 1)
                if mid == TOPK:
                    n = 3 * (g - LAST)
                    dve.sem_inc(taken, 1)
                    for t in range(T):
                        last = dve.max(top_a[:, t, :], attn[:, t, :])
                    last.then_inc(top_step, 1)
                    dve.wait_ge(top_step, n + 1)
                    dve.sem_inc(taken, 1)
                    for t in range(T):
                        last = dve.match_replace(masked[:, t, :], top_a[:, t, :], attn[:, t, :], -1.0)
                    last.then_inc(top_step, 1)
                    dve.wait_ge(top_step, n + 2)
                    dve.sem_inc(taken, 1)
                    for t in range(T):
                        last = dve.max(top_b[:, t, :], masked[:, t, :])
                    last.then_inc(top_step, 1)
                    dve.wait_ge(top_step, n + 3)
                dve.reciprocal(inv_sum[:, :], row_sum[:, :]).then_inc(inv_ready, 1)
                if mid == TOPK:
                    for t in range(T):
                        last = dve.scalar_tensor_tensor(out=attn[:, t, :], in0=attn[:, t, :], scalar=top_b[:, t, 7:8],
                                                        in1=attn[:, t, :], op0=ALU.is_ge, op1=ALU.mult)
                    last.then_inc(attn_ready, 1)
                else:
                    dve.sem_inc(attn_ready, 1)

            def copy_attnT(g):
                dve.wait_ge(attn_turned, 2 * g + 2)
                if known(g):
                    dve.wait_ge(mixed, 2 * g)
                dve.tensor_copy(attnT[:, 1, :, :].rearrange("p a n -> p (a n)"), TR[1][:, :]).then_inc(attnT_d, 1)

            def keep_inverse(g, b):
                dve.wait_ge(inv_ready, g + 1)
                if b in PROJ and known(g):
                    dve.wait_ge(elu_exp, proj_unit(g, b))
                dve.tensor_copy(inv_late[:, :], inv_sum[:, :]).then_inc(inv_kept, 1)

            def elu_first(g, b):
                a = proj_unit(g, b)
                dve.wait_ge(elu_pos, a + 1)
                dve.wait_ge(xm_in, 16 * (g + 1))
                dve.scalar_tensor_tensor(out=elu_r[:, :, :], in0=elu_r[:, :, :], scalar=-1.0, in1=x_mix[:, :, :],
                                         op0=ALU.add, op1=ALU.add).then_inc(elu_sum, 1)

            def residual(g, before, b):
                if before in FFN:
                    dve.wait_ge(res_scaled, g - FFN0)
                elif before == BLOCKS - 2:
                    dve.wait_ge(normed[0], g)
                elif before == BLOCKS - 1:
                    dve.wait_ge(out_saved, 16 * (g - LAST))
                elif before is not None:
                    if k_is(g, PAIRS):
                        dve.wait_ge(normed[0], g)
                    else:
                        dve.wait_ge(y_saved, 16 * g)
                        dve.wait_ge(outer_saved, 16 * g)
                if k_is(g, 0):
                    dve.wait_ge(bb_ready, 1)
                if b in PROJ:
                    a = proj_unit(g, b)
                    dve.wait_ge(elu_exp, a + 1)
                    dve.wait_ge(elu_sum, a + 1)
                    dve.scalar_tensor_tensor(out=y[:, :, :], in0=elu_e[:, :, :], scalar=1.0, in1=elu_r[:, :, :],
                                             op0=ALU.min, op1=ALU.add).then_inc(y_ready, 1)
                else:
                    if b in FFN:
                        dve.wait_ge(inv_ready, g + 1)
                    else:
                        dve.wait_ge(inv_kept, y_store(g, b) + 1)
                    inv = inv_sum if b in FFN else inv_late
                    mix_banks = banks(before, b)[0]
                    dve.wait_ge(xm_in, 16 * (g + 1))
                    for t in range(T):
                        if t % 2 == 0:
                            dve.wait_ge(mixed, 2 * g + t // 2 + 1)
                        last = dve.scalar_tensor_tensor(out=y[:, t, :], in0=mix_banks[t // 2][:, (t % 2) * D:(t % 2 + 1) * D],
                                                        scalar=inv[:, t:t + 1], in1=x_mix[:, t, :],
                                                        op0=ALU.mult, op1=ALU.add)
                    last.then_inc(y_ready, 1)

            def moments_of_y(g):
                dve.wait_ge(y_ready, g + 1)
                layer_norm(0, g, y)

            def split_h(g):
                f = g - FFN0
                for u in range(KT):
                    dve.wait_ge(hT_ready, 2 * f + u + 1)
                    if known(f) and u == 0:
                        dve.wait_ge(hid_done, FT * f)
                    dve.tensor_copy(h_hi[:, u, :], hT[:, u, :]).then_inc(h_hi_ready, 1)
                    dve.wait_ge(h_hi_ready, 2 * f + u + 1)
                    dve.tensor_tensor(h_lo[:, u, :], hT[:, u, :], h_hi[:, u, :].bitcast(F32), ALU.subtract)\
                        .then_inc(h_ready, 1)

            def split_act(k, ft):
                f = k - FFN0
                dve.wait_ge(act_ready, FT * f + ft + 1)
                if ft >= 4 or known(f):
                    dve.wait_ge(ff_done, FT * f + ft - 3)
                dve.tensor_tensor(act_lo[:, ft % 4, :], act[:, ft % 2, :], act_hi[:, ft % 4, :].bitcast(F32),
                                  ALU.subtract).then_inc(act_split, 1)

            def step(k, prev, cur, mid, front):
                if isinstance(k, int) and k % PAIRS == PAIRS - 2 and 0 < k and k // PAIRS + 1 in range(2, BLOCKS):
                    prepare(k // PAIRS + 1)
                if cur is not None and cur not in FFN:
                    keep_inverse(k, cur)
                f1 = k - 1 - FFN0
                n = k - 1 - FFN[-1] * PAIRS
                inner = cur in FFN and mid in FFN
                new_layer = cur in FFN and cur != FFN[0] and k_is(k, cur * PAIRS)
                last_unit = inner and k_is(k, cur * PAIRS + PAIRS - 1)
                s_bank, d_bank = banks(cur, mid)[1:]

                def sum_layer():
                    dve.wait_ge(ff_done, FT * (f1 + 1))
                    dve.wait_ge(res_ready, f1 + 1)
                    if prev == FFN[-1] and not k_is(k, FFN[-1] * PAIRS + 1):
                        dve.wait_ge(normed[2], n)
                    elif known(f1):
                        dve.wait_ge(y2_saved, 16 * f1)
                    for c in range(2):
                        last = dve.tensor_tensor(y2[:, 2 * c:2 * c + 2, :].rearrange("p a n -> p (a n)"), ACC[c][:, :],
                                                 h_res[:, 2 * c:2 * c + 2, :].rearrange("p a n -> p (a n)"), ALU.add)
                    last.then_inc(y2_ready, 1)

                def moments_of_layer():
                    dve.wait_ge(y2_ready, f1 + 1)
                    layer_norm(1, f1, y2)

                if prev in FFN:
                    sum_layer()
                    if not inner:
                        moments_of_layer()
                if mid is not None:
                    weights(k + 1, mid)
                if new_layer:
                    dve.wait_ge(ff_done, FT * (k - FFN0))
                    next_quarter(cur - 1, 2)
                if cur in FFN:
                    split_act(k, 0)
                    split_act(k, 1)
                if inner and prev in FFN:
                    moments_of_layer()
                elif prev in FFN:
                    finish(1, f1, y2)
                if k_is(k, 0):
                    dve.wait_ge(vec_mm, 1)
                    dve.tensor_copy(vec[:, :], TR[0][:, 0:V_ROWS]).then_inc(vec_ready, 1)
                    dve.wait_ge(vec_ready, 1)
                    prepare(1)
                if cur in PROJ:
                    elu_first(k, cur)
                elif cur is not None and cur not in FFN:
                    residual(k, prev, cur)
                if cur == TOPK:
                    residual(k, prev, cur)
                if cur in FFN and not inner:
                    for ft in range(2, 5):
                        split_act(k, ft)
                if mid is not None and not inner:
                    copy_attnT(k + 1)
                if inner:
                    split_act(k, 2)
                    split_act(k, 3)
                    if prev in FFN:
                        dve.wait_ge(rstd_ready[1], f1 + 1)
                        if known(f1):
                            dve.wait_ge(normed[1], f1)
                        dve.scalar_tensor_tensor(out=shift[:, :], in0=mean_var[1][:, :, 0], scalar=-1.0, in1=rstd[1][:, :],
                                                 op0=ALU.mult, op1=ALU.mult).then_inc(shift_ready, 1)
                    if by_rows(k + 2, front):
                        row_sums(k + 2, front)
                    split_act(k, 4)
                    if new_layer:
                        next_quarter(cur - 1, 3)
                early = mid not in FFN and front is not None
                if early and cur not in FFN:
                    scores(k + 2, front, s_bank, d_bank)
                if cur == 0:
                    residual(k, prev, cur)
                if cur is not None and cur not in FFN:
                    moments_of_y(k)
                if k_is(k, PAIRS - 1):
                    dve.wait_ge(mixed, 2 * PAIRS)
                if cur in PROJ:
                    finish(0, k, y, values if k_is(k, PAIRS - 1) else y)
                elif cur is not None and cur not in FFN:
                    if known(k, 4 * PAIRS + 1):
                        dve.wait_ge(y_saved, 16 * y_store(k, cur))
                    finish(0, k, y, normed_avg)
                if mid in FFN:
                    residual(k + 1, cur, mid)
                    moments_of_y(k + 1)
                if prev == FFN[-1]:
                    dve.wait_ge(outer_added, n + 1)
                    layer_norm(2, n, y2)
                if cur in FFN:
                    split_act(k, 5)
                if mid in FFN:
                    finish(0, k + 1, y)
                if cur in FFN:
                    split_act(k, 6)
                    split_act(k, 7)
                if last_unit:
                    dve.wait_ge(hid_done, FT * (k - FFN0 + 1))
                    next_quarter(cur, 0)
                if mid in FFN:
                    scores(k + 2, front, s_bank, d_bank)
                    split_h(k + 1)
                if last_unit:
                    next_quarter(cur, 1)
                if k_is(k, -1):
                    for q in range(4):
                        split_quarter(0, q, first_raw[q], 1, q)
                if prev == FFN[-1]:
                    finish(2, n, y2, x_saved)
                if cur in FFN and not inner:
                    scores(k + 2, front, s_bank, d_bank)

            drive(dve, step)

        @block.tensor
        def _(pe):
            pe.wait_ge(ident_ready, 2)

            def hidden(k, ft, inner):
                f = k - FFN0
                if ft >= 4 or known(f):
                    pe.wait_ge(act_ready, FT * f + ft - 3)
                if ft >= 6 and inner:
                    pe.wait_ge(y_ready, k + 2)
                if ft == (2 if k_is(k, FFN0) else 0):
                    pe.wait_ge(s_ready, k + 2)
                if ft == (3 if k_is(k, FFN0) else 1):
                    pe.wait_ge(max_ready, k + 2)
                o = HID[ft % 4][:, :]
                for c in range(KT):
                    if ft == 0:
                        pe.wait_ge(h_ready, 2 * f + c + 1)
                    if ft == 0 and isinstance(k, int) and k % PAIRS == 0:
                        pe.wait_ge(chunk_split, 4 * (k // PAIRS - 1) + c + 1)
                    col = slice(ft * P, (ft + 1) * P)
                    pe.matmul(o, w1_hi[:, c, col], h_hi[:, c, :], start=(c == 0), stop=False)
                    pe.matmul(o, w1_hi[:, c, col], h_lo[:, c, :], start=False, stop=False)
                    last = pe.matmul(o, w1_lo[:, c, col], h_hi[:, c, :], start=False, stop=(c == KT - 1))
                last.then_inc(hid_done, 1)

            def down(k, ft):
                f = k - FFN0
                pe.wait_ge(act_split, FT * f + ft + 1)
                if ft == 0 and known(f):
                    pe.wait_ge(y2_ready, f)
                for t in range(T):
                    o = ACC[t // 2][:, (t % 2) * D:(t % 2 + 1) * D]
                    col = slice(t * P, (t + 1) * P)
                    pe.matmul(o, act_hi[:, ft % 4, col], w2_hi[:, ft, :], start=(ft == 0 and t % 2 == 0), stop=False,
                              skip_group_check=True)
                    pe.matmul(o, act_hi[:, ft % 4, col], w2_lo[:, ft, :], start=False, stop=False, skip_group_check=True)
                    last = pe.matmul(o, act_lo[:, ft % 4, col], w2_hi[:, ft, :], start=False, stop=(ft == FT - 1),
                                     skip_group_check=True)
                last.then_inc(ff_done, 1)

            def turn_attn(g):
                pe.wait_ge(attn_ready, g + 1)
                for u in range(2):
                    for j in range(KT):
                        for i in range(KT):
                            last = pe.transpose(TR[u][:, (j * KT + i) * P:(j * KT + i + 1) * P],
                                                attn[:, u * KT + i, j * P:(j + 1) * P], ident[:, :])
                    last.then_inc(attn_turned, 1)

            def mix(k, g, cur, mid, u):
                if u == 0:
                    if mid in PROJ:
                        pe.wait_ge(values_ready, 2 * (proj_unit(g, mid) + 1))
                    elif own_values(g, mid):
                        pe.wait_ge(av_in, 16 * (g - AVG_FIRST + 1))
                    else:
                        pe.wait_ge(xm_in, 16 * (g + 1))
                    if cur in FFN:
                        pe.wait_ge(act_ready, FT * (k - FFN0) + (4 if mid in FFN else 6))
                    elif cur in PROJ:
                        pe.wait_ge(elu_exp, proj_unit(k, cur) + 1)
                    elif cur is not None:
                        pe.wait_ge(y_ready, g)
                v = values if mid in PROJ or own_values(g, mid) else x_mix
                pe.wait_ge(attnT_a if u == 0 else attnT_d, g + 1)
                for i in range(KT):
                    for j in range(KT):
                        last = pe.matmul(banks(cur, mid)[0][u][:, i * D:(i + 1) * D], attnT[:, u, j, i * P:(i + 1) * P],
                                         v[:, u * KT + j, :], start=(j == 0), stop=(j == KT - 1))
                last.then_inc(mixed, 1)

            def turn_x(g, near, after=None):
                if isinstance(g, int) and g >= UNITS or by_rows(g, near):
                    return
                pe.wait_ge(xs_in, 16 * (g + 1))
                if after is not None:
                    pe.wait_ge(attnT_a, after + 1)
                    pe.wait_ge(attnT_d, after + 1)
                elif known(g):
                    pe.wait_ge(xT_ready, 2 * s_unit(g, near))
                for u in range(KT):
                    for t in range(T):
                        last = pe.transpose(TR[u][:, t * P:(t + 1) * P], x_front[:, t, u * P:(u + 1) * P], ident[:, :])
                    last.then_inc(x_turned, 1)

            def target_scores(k, g, cur, front, bank):
                if by_rows(g, front):
                    pe.wait_ge(d_summed, g + 1 - ROW_FIRST)
                else:
                    pe.wait_ge(xT_ready, 2 * (s_unit(g, front) + 1))
                if isinstance(g, int) and g % PAIRS == 0:
                    pe.wait_ge(prep_ready, g // PAIRS + 1)
                if cur in FFN:
                    pe.wait_ge(act_ready, FT * (k - FFN0) + (FT if bank is HID[3] else 6))
                elif known(g):
                    pe.wait_ge(max_ready, g)
                for t in range(T if by_rows(g, front) else 0):
                    last = pe.matmul(bank[:, t * P:(t + 1) * P], d_sum[:, t:t + 1].to_broadcast([P, P]), ident[:, :],
                                     start=True, stop=True)
                for c in range(0 if by_rows(g, front) else KT):
                    last = pe.matmul(bank[:, :], dst_rep[:, front % 2, c, :], xT[:, c, :], start=(c == 0),
                                     stop=(c == KT - 1))
                last.then_inc(scored, 1)

            def source_scores(k, g, cur, front, bank):
                if cur in FFN:
                    pe.wait_ge(act_ready, FT * (k - FFN0) + (FT - 1 if bank is HID[2] else 5))
                elif known(g):
                    pe.wait_ge(s_ready, g)
                for t in range(T):
                    for c in range(KT):
                        last = pe.matmul(bank[:, t:t + 1], xT[:, c, t * P:(t + 1) * P], columns(front, 0)[:, c:c + 1],
                                         start=(c == 0), stop=(c == KT - 1))
                last.then_inc(s_scored, 1)

            def project(k, g, front):
                a = proj_unit(g, front)
                pe.wait_ge(xT_ready, 2 * (s_unit(g, front) + 1))
                if known(a):
                    pe.wait_ge(values_ready, 2 * a)
                if front == 0 and isinstance(g, int) and g == 0:
                    pe.wait_ge(prep_ready, 1)
                if front == TOPK and isinstance(g, int):
                    pe.wait_ge(prep_ready, TOPK + 1)
                    pe.wait_ge(y2_ready, 3 * PAIRS)
                for t in range(T):
                    for c in range(KT):
                        last = pe.matmul(ACC[t // 2][:, (t % 2) * D:(t % 2 + 1) * D], xT[:, c, t * P:(t + 1) * P],
                                         w_proj[:, c, :], start=(c == 0), stop=(c == KT - 1))
                last.then_inc(projected, 1)

            def step(k, prev, cur, mid, front):
                g, g2 = k + 1, k + 2
                s_bank, d_bank = banks(cur, mid)[1:]
                inner = cur in FFN and mid in FFN
                if cur in FFN:
                    for ft in range(5):
                        hidden(k, ft, inner)
                    if k_is(k, cur * PAIRS):
                        pe.wait_ge(chunk_split, 4 * (cur - 1) + 3)
                    down(k, 0)
                if inner:
                    turn_attn(g)
                    hidden(k, 5, inner)
                    down(k, 1)
                    mix(k, g, cur, mid, 0)
                    mix(k, g, cur, mid, 1)
                    down(k, 2)
                    turn_x(g2, front, g)
                    down(k, 3)
                    hidden(k, 6, inner)
                    hidden(k, 7, inner)
                    target_scores(k, g2, cur, front, d_bank)
                    if not by_rows(g2, front):
                        source_scores(k, g2, cur, front, s_bank)
                    if k_is(k, cur * PAIRS):
                        pe.wait_ge(chunk_split, 4 * cur)
                    down(k, 4)
                    down(k, 5)
                elif cur in FFN:
                    hidden(k, 5, inner)
                    down(k, 1)
                    hidden(k, 6, inner)
                    down(k, 2)
                    turn_attn(g)
                    hidden(k, 7, inner)
                    mix(k, g, cur, mid, 0)
                    mix(k, g, cur, mid, 1)
                    for ft in range(3, 6):
                        down(k, ft)
                    turn_x(g2, front, g)
                    down(k, 6)
                    down(k, 7)
                    target_scores(k, g2, cur, front, d_bank)
                    source_scores(k, g2, cur, front, s_bank)
                    turn_x(k + 3, front)
                else:
                    if k_is(k, -2):
                        turn_x(0, 0)
                    if front is not None:
                        target_scores(k, g2, cur, front, d_bank)
                    if front in PROJ:
                        project(k, g2, front)
                    if front in (4, 5):
                        source_scores(k, g2, cur, front, s_bank)
                    if k_is(k, 0):
                        pe.wait_ge(consts_in, 16 * CONSTS)
                        pe.transpose(TR[0][:, 0:V_ROWS], vec_rows[:, :], ident[0:V_ROWS, 0:V_ROWS]).then_inc(vec_mm, 1)
                        pe.wait_ge(vec_ready, 1)
                    if mid is not None:
                        turn_attn(g)
                    if front in (0, 1):
                        source_scores(k, g2, cur, front, s_bank)
                    if mid is not None:
                        mix(k, g, cur, mid, 0)
                    if mid not in FFN:
                        turn_x(k + 3, front, None if mid is None else g)
                    if mid is not None:
                        mix(k, g, cur, mid, 1)
                if mid in FFN:
                    pe.wait_ge(normed[0], g + 1)
                    if cur in FFN:
                        if by_rows(g2, front):
                            pe.wait_ge(attnT_a, g + 1)
                            pe.wait_ge(attnT_d, g + 1)
                        else:
                            pe.wait_ge(xT_ready, 2 * (s_unit(g2, front) + 1))
                    for u in range(KT):
                        for t in range(T):
                            last = pe.transpose(TR[u][:, t * P:(t + 1) * P], y[:, t, u * P:(u + 1) * P], ident[:, :])
                        last.then_inc(n_turned, 1)
                if inner:
                    down(k, 6)
                    down(k, 7)

            drive(pe, step)


_INS = ['x', 'adj', 'L0_gnn_w', 'L0_gnn_a1', 'L0_gnn_a2', 'L1_gnn_attn_w', 'L1_gnn_attn_b', 'L1_gnn_W1', 'L1_gnn_b1',
        'L1_gnn_W2', 'L1_gnn_b2', 'L1_gnn_g1', 'L1_gnn_beta1', 'L1_gnn_g2', 'L1_gnn_beta2', 'L2_gnn_attn_w_src',
        'L2_gnn_attn_w_dst', 'L2_gnn_attn_b', 'L3_gnn_W', 'L3_gnn_a']
_OUTS = [((GRAPHS, N, D), 'float32')]


def kernel(**inputs):
    import numpy as _np
    import concourse.bacc as _bacc
    from concourse import mybir as _mybir
    from concourse.bass_utils import run_bass_kernel_spmd as _run

    nc = _bacc.Bacc("TRN2", target_bir_lowering=False, num_devices=1)
    arrays, args = {}, []
    for name in _INS:
        a = _np.ascontiguousarray(inputs[name])
        arrays[f"in_{name}_dram"] = a
        args.append(nc.dram_tensor(f"in_{name}_dram", a.shape, _mybir.dt.from_np(a.dtype), kind="ExternalInput").ap())
    for i, (shape, dtype) in enumerate(_OUTS):
        dt = _mybir.dt.from_np(_np.dtype(dtype))
        args.append(nc.dram_tensor(f"out_{i}_dram", shape, dt, kind="ExternalOutput").ap())
    graph_stack(nc, *args)
    r = _run(nc, [arrays], core_ids=[0])
    got = tuple(r.results[0][f"out_{i}_dram"] for i in range(len(_OUTS)))
    return got[0]
```
